# Optimizing a Trainium2 kernel written in Bass

```python
import numpy as np
import jax
import jax.numpy as jnp

def _softmax(x, axis=-1):
    return jax.nn.softmax(x, axis=axis)

def _gelu(x):
    return jax.nn.gelu(x, approximate=True)

def _silu(x):
    return jax.nn.silu(x)

def _sigmoid(x):
    return jax.nn.sigmoid(x)

def _layernorm(x, axis=-1, eps=1e-05):
    m = jnp.mean(x, axis=axis, keepdims=True)
    v = jnp.var(x, axis=axis, keepdims=True)
    return (x - m) / jnp.sqrt(v + eps)

def _scatter_add(tgt, idx, src, axis=0):
    return tgt.at[idx].add(src)

def _segment_sum(src, seg, n):
    return jax.ops.segment_sum(src, seg, n)
kernel_name = 'mk_prb_d1_jaxref_r8_cccf64'

def setup_inputs(seed: int=0):
    np.random.seed(seed)
    _w = jnp.asarray

    def _L0_attn_setup():
        import jax, jax.numpy as jnp
        import numpy as np
        HIDDEN = 256
        NUM_HEADS = 16
        Q_A_RANK = 192
        KV_A_RANK = 64
        Q_NOPE = 128
        Q_ROPE = 64
        Q_HEAD = Q_NOPE + Q_ROPE
        V_HEAD = 128
        K_PE = Q_ROPE
        ROPE_THETA = 10000.0
        ROPE_SCALE = 1.0
        EPS = 1e-06

        def rms_norm(x, w):
            var = jnp.mean(jnp.square(x), axis=-1, keepdims=True)
            return x * jax.lax.rsqrt(var + EPS) * w

        def rotate_half(x):
            x1, x2 = jnp.split(x, 2, axis=-1)
            return jnp.concatenate([-x2, x1], axis=-1)

        def apply_rotary(x, cos, sin):
            return x * cos + rotate_half(x) * sin
        key = jax.random.key(seed)
        ks = jax.random.split(key, 9)

        def init(k, shape):
            fan_in = shape[0]
            return (jax.random.normal(k, shape, dtype=jnp.float32) / np.sqrt(fan_in)).astype(jnp.float32)
        B, S = (2, 256)
        return {'h': jax.random.normal(ks[0], (B, S, HIDDEN), dtype=jnp.float32), 'w_q_a': init(ks[1], (HIDDEN, Q_A_RANK)), 'g_q_a': jnp.ones((Q_A_RANK,), dtype=jnp.float32), 'w_q_b': init(ks[2], (Q_A_RANK, NUM_HEADS * Q_HEAD)), 'w_kv_a': init(ks[3], (HIDDEN, KV_A_RANK + K_PE)), 'g_kv_a': jnp.ones((KV_A_RANK,), dtype=jnp.float32), 'w_kv_b': init(ks[4], (KV_A_RANK, NUM_HEADS * (Q_NOPE + V_HEAD))), 'w_o': init(ks[5], (NUM_HEADS * V_HEAD, HIDDEN))}
    _L0_attn_in = _L0_attn_setup()

    def _L0_ffn_setup():
        import jax, jax.numpy as jnp
        import numpy as np
        B, S, H = (2, 128, 256)
        E, K, F = (64, 8, 96)
        CAP = 64
        key = jax.random.key(seed)
        k1, k2, k3, k4, k5 = jax.random.split(key, 5)
        scale_h = 1.0 / np.sqrt(H)
        scale_f = 1.0 / np.sqrt(F)
        return {'hidden_states': jax.random.normal(k1, (B, S, H), jnp.float32), 'router_w': jax.random.normal(k2, (E, H), jnp.float32) * scale_h, 'w_gate': jax.random.normal(k3, (E, H, F), jnp.float32) * scale_h, 'w_up': jax.random.normal(k4, (E, H, F), jnp.float32) * scale_h, 'w_down': jax.random.normal(k5, (E, F, H), jnp.float32) * scale_f}
    _L0_ffn_in = _L0_ffn_setup()
    _d = {'L0_attn_h': _L0_attn_in['h'], 'L0_attn_w_q_a': _L0_attn_in['w_q_a'], 'L0_attn_g_q_a': _L0_attn_in['g_q_a'], 'L0_attn_w_q_b': _L0_attn_in['w_q_b'], 'L0_attn_w_kv_a': _L0_attn_in['w_kv_a'], 'L0_attn_g_kv_a': _L0_attn_in['g_kv_a'], 'L0_attn_w_kv_b': _L0_attn_in['w_kv_b'], 'L0_attn_w_o': _L0_attn_in['w_o'], 'L0_ffn_router_w': _L0_ffn_in['router_w'], 'L0_ffn_w_gate': _L0_ffn_in['w_gate'], 'L0_ffn_w_up': _L0_ffn_in['w_up'], 'L0_ffn_w_down': _L0_ffn_in['w_down']}
    _x0 = _d['L0_attn_h']
    _d['L0_attn_h'] = jax.random.normal(jax.random.fold_in(jax.random.key(seed), 1), (4, 512, 256), dtype=_x0.dtype)
    del _x0
    return _d

def reference(L0_attn_h, L0_attn_w_q_a, L0_attn_g_q_a, L0_attn_w_q_b, L0_attn_w_kv_a, L0_attn_g_kv_a, L0_attn_w_kv_b, L0_attn_w_o, L0_ffn_router_w, L0_ffn_w_gate, L0_ffn_w_up, L0_ffn_w_down):

    def _L0_attn_ref(h, w_q_a, g_q_a, w_q_b, w_kv_a, g_kv_a, w_kv_b, w_o):
        import jax, jax.numpy as jnp
        import numpy as np
        HIDDEN = 256
        NUM_HEADS = 16
        Q_A_RANK = 192
        KV_A_RANK = 64
        Q_NOPE = 128
        Q_ROPE = 64
        Q_HEAD = Q_NOPE + Q_ROPE
        V_HEAD = 128
        K_PE = Q_ROPE
        ROPE_THETA = 10000.0
        ROPE_SCALE = 1.0
        EPS = 1e-06

        def rms_norm(x, w):
            var = jnp.mean(jnp.square(x), axis=-1, keepdims=True)
            return x * jax.lax.rsqrt(var + EPS) * w

        def rotate_half(x):
            x1, x2 = jnp.split(x, 2, axis=-1)
            return jnp.concatenate([-x2, x1], axis=-1)

        def apply_rotary(x, cos, sin):
            return x * cos + rotate_half(x) * sin
        B, S, _ = h.shape
        H = NUM_HEADS
        q_a = rms_norm(h @ w_q_a, g_q_a)
        q = (q_a @ w_q_b).reshape(B, S, H, Q_HEAD).transpose(0, 2, 1, 3)
        q_nope, q_pe = (q[..., :Q_NOPE], q[..., Q_NOPE:])
        kv_a = h @ w_kv_a
        kv_nope, k_pe = (kv_a[..., :KV_A_RANK], kv_a[..., KV_A_RANK:])
        kv_nope = rms_norm(kv_nope, g_kv_a)
        kv = (kv_nope @ w_kv_b).reshape(B, S, H, Q_NOPE + V_HEAD).transpose(0, 2, 1, 3)
        k_nope, v = (kv[..., :Q_NOPE], kv[..., Q_NOPE:])
        t = jnp.arange(S, dtype=jnp.float32) / ROPE_SCALE
        inv_freq = 1.0 / ROPE_THETA ** (jnp.arange(0, Q_ROPE, 2, dtype=jnp.float32) / Q_ROPE)
        freqs = t[:, None] * inv_freq[None, :]
        emb = jnp.concatenate([freqs, freqs], axis=-1)
        cos = jnp.cos(emb)[None, None]
        sin = jnp.sin(emb)[None, None]
        q_pe = apply_rotary(q_pe, cos, sin)
        k_pe = apply_rotary(k_pe[:, None, :, :], cos, sin)
        k_pe = jnp.broadcast_to(k_pe, (B, H, S, K_PE))
        q_full = jnp.concatenate([q_nope, q_pe], axis=-1)
        k_full = jnp.concatenate([k_nope, k_pe], axis=-1)
        scale = 1.0 / np.sqrt(Q_HEAD)
        attn = jnp.einsum('bhqd,bhkd->bhqk', q_full, k_full) * scale
        causal = jnp.tril(jnp.ones((S, S), dtype=bool))
        attn = jnp.where(causal[None, None], attn, -jnp.inf)
        attn_weights = jax.nn.softmax(attn, axis=-1)
        out = jnp.einsum('bhqk,bhkd->bhqd', attn_weights, v)
        out = out.transpose(0, 2, 1, 3).reshape(B, S, H * V_HEAD)
        return out @ w_o

    def _L0_ffn_ref(hidden_states, router_w, w_gate, w_up, w_down):
        import jax, jax.numpy as jnp
        import numpy as np
        B, S, H = (2, 128, 256)
        E, K, F = (64, 8, 96)
        CAP = 64
        b, s, h = hidden_states.shape
        T = b * s
        xf = hidden_states.reshape(T, h)
        logits = xf @ router_w.T
        scores = jax.nn.softmax(logits.astype(jnp.float32), axis=-1)
        topk_w, topk_idx = jax.lax.top_k(scores, K)
        topk_w = topk_w / (topk_w.sum(axis=-1, keepdims=True) + 1e-20)
        slot_expert = topk_idx.reshape(-1)
        slot_token = jnp.repeat(jnp.arange(T), K)
        onehot = jax.nn.one_hot(slot_expert, E, dtype=jnp.int32)
        pos = (jnp.cumsum(onehot, axis=0) * onehot).sum(-1) - 1
        valid = pos < CAP
        dest = jnp.where(valid, slot_expert * CAP + pos, E * CAP)
        buf = jnp.zeros((E * CAP + 1, h), xf.dtype).at[dest].set(xf[slot_token])
        xb = buf[:E * CAP].reshape(E, CAP, h)
        gate = jnp.einsum('ech,ehf->ecf', xb, w_gate)
        up = jnp.einsum('ech,ehf->ecf', xb, w_up)
        hmid = jax.nn.silu(gate) * up
        yb = jnp.einsum('ecf,efh->ech', hmid, w_down).reshape(E * CAP, h)
        yb = jnp.concatenate([yb, jnp.zeros((1, h), yb.dtype)], axis=0)
        slot_out = yb[dest] * topk_w.reshape(-1)[:, None].astype(yb.dtype)
        out = jnp.zeros((T, h), yb.dtype).at[slot_token].add(slot_out)
        return out.reshape(b, s, h)
    x = L0_attn_h
    xn = _layernorm(x, axis=-1)
    x = x + _L0_attn_ref(xn, L0_attn_w_q_a, L0_attn_g_q_a, L0_attn_w_q_b, L0_attn_w_kv_a, L0_attn_g_kv_a, L0_attn_w_kv_b, L0_attn_w_o) + _L0_ffn_ref(xn, L0_ffn_router_w, L0_ffn_w_gate, L0_ffn_w_up, L0_ffn_w_down)
    return x

_drawn_inputs = setup_inputs


def setup_inputs(seed=0):
    import zlib

    import numpy as np

    out = dict(_drawn_inputs(seed))
    spreads = {'L0_attn_g_q_a': (1.0, 0.2), 'L0_attn_g_kv_a': (1.0, 0.2)}
    factors = {}
    for name, (base, spread) in spreads.items():
        noise = np.random.default_rng([zlib.crc32(name.encode()), seed]).standard_normal(out[name].shape)
        drawn = base * np.exp(spread * noise) if base else spread * noise
        out[name] = jnp.asarray(drawn.astype(out[name].dtype))
    for name, factor in factors.items():
        out[name] = (out[name] * factor).astype(out[name].dtype)
    return out
```

```python
from contextlib import ExitStack

import concourse.bass as bass
from concourse import mybir

ALU = mybir.AluOpType
ACT = mybir.ActivationFunctionType
AX = mybir.AxisListType
F32 = mybir.dt.float32
F16 = mybir.dt.float16
BF16 = mybir.dt.bfloat16
U32 = mybir.dt.uint32

P = 128
B, S, H = 4, 512, 256
T = B * S
NH, NOPE, ROPE, VD = 16, 128, 64, 128
RQ, RK = 192, 64
E, TOPK, F, CAP = 64, 8, 96, 64
NB = T // P
QB = S // P
HP = NH // 2
NC = H // P
SCALE = float((NOPE + ROPE) ** -0.5)
LN_EPS, RMS_EPS = 1e-5, 1e-6

A_DUP, A_KV, A_PE, A_RT, A_W = RQ, RQ + 64, RQ + 64 + RK, RQ + 64 + RK + ROPE, RQ + 64 + RK + ROPE + E

R_WT, R_ID, R_W = H, H + E, H + E + 1
SLOTS = E * CAP
MROWS = T + CAP

C_COS, C_SIN, C_ID, C_KEY, C_TOK, C_OFF, C_DEF, C_MASK, C_TRI, C_W = (
    0, 256, 512, 640, 704, 720, 721, 722, 850, 978)

IORDER = [3, 2, 1, 0]
UNITS = B * QB
PAIRS = E // 2
NSC = NB * TOPK


def table():
    import numpy as np

    c = np.zeros((P, C_W), np.float32)
    pos = np.arange(S, dtype=np.float32)
    inv = (1.0 / np.float32(10000.0) ** (np.arange(0, ROPE, 2, dtype=np.float32) / np.float32(ROPE))).astype(np.float32)
    ang = (pos[:, None] * inv[None, :]).astype(np.float32)
    cos, sin = np.cos(ang).astype(np.float32), np.sin(ang).astype(np.float32)
    for i in range(QB):
        rows = slice(i * P, (i + 1) * P)
        c[:, C_COS + i * 64:C_COS + (i + 1) * 64] = np.concatenate([cos[rows], cos[rows]], 1)
        c[:, C_SIN + i * 64:C_SIN + (i + 1) * 64] = np.concatenate([-sin[rows], sin[rows]], 1)
    p = np.arange(P)
    c[:, C_ID:C_ID + P] = np.eye(P)
    c[:, C_KEY:C_KEY + E] = SLOTS - CAP * np.arange(E)[None, :]
    c[:, C_TOK:C_TOK + NB] = p[:, None] + P * np.arange(NB)[None, :]
    c[:, C_OFF] = np.where(p < CAP, 0, MROWS)
    c[:, C_DEF] = T + p % CAP
    c[:, C_MASK:C_MASK + P] = np.where(p[None, :] > p[:, None], -1e30, 0.0)
    c[:, C_TRI:C_TRI + P] = p[:, None] < p[None, :]
    return c


def mla_moe_kernel(nc, h, w_q_a, g_q_a, w_q_b, w_kv_a, g_kv_a, w_kv_b, w_o, router_w, w_gate, w_up,
                   w_down, consts, out):
    x_d = h.rearrange("b (i p) n -> p (b i) n", p=P)
    out_d = out.rearrange("b (i p) n -> p (b i) n", p=P)
    slots_d = nc.dram_tensor("expert_slots", [SLOTS, R_W], F32, kind="Internal").ap()
    moe_d = nc.dram_tensor("moe_sums", [2 * MROWS, H], F32, kind="Internal").ap()

    with ExitStack() as ctx:
        def sb(name, shape, dt):
            return ctx.enter_context(nc.sbuf_tensor(name, shape, dt))

        def sem(name):
            return ctx.enter_context(nc.semaphore(name))

        qreg = sb("queries", [P, B * HP * 2 * 2 * S], F16)
        Q = qreg[:, :].rearrange("p (b h s l q) -> p b h s l q", b=B, h=HP, s=2, l=2)
        KT = sb("keys_t", [P, 2, T], F16)
        V = sb("values", [P, NB, RK], F32)
        WVO = sb("w_values_out", [P, 2, HP, H], F16)
        cst = sb("constants", [P, C_MASK], F32)
        ident = cst[:, C_ID:C_ID + P]
        identb = sb("identity_bf16", [P, P], BF16)
        maskb = sb("causal_mask", [P, P], BF16)
        trib = sb("earlier_token", [P, P], BF16)
        onesb = sb("ones_bf16", [P, P], BF16)
        small = sb("small", [P, 64], F32)

        early = qreg[:, :].bitcast(F32)
        at = [0]

        def room(n):
            a = early[:, at[0]:at[0] + n]
            at[0] += n
            return a

        xnT = room(NC * T).rearrange("p (c t) -> p c t", c=NC)
        x_sb = room(NB * H).rearrange("p (j n) -> p j n", n=H)
        WQ0 = room(NH * RQ).rearrange("p (h n) -> p h n", h=NH)
        WQ1 = room(NH * RQ).rearrange("p (h n) -> p h n", h=NH)
        WKV = room(NH * 256).rearrange("p (h n) -> p h n", h=NH)
        WO = room(NH * H).rearrange("p (h n) -> p h n", h=NH)
        AL = room(NB * A_W).rearrange("p (j n) -> p j n", n=A_W)
        WA = room(NC * A_W).rearrange("p (c n) -> p c n", c=NC)
        rt_row = room(H)
        late_c = room(2 * P)
        bn6 = room(NB * 6).rearrange("p (j n) -> p j n", n=6)
        mv = room(NB * 2).rearrange("p (j n) -> p j n", n=2)
        ve, sd, rs, nt = (room(NB) for _ in range(4))
        ssq, rv, rsd, rr, rt = (room(2 * NB).rearrange("p (a j) -> p a j", a=2) for _ in range(5))
        gq = room(2)
        gs = room(2)
        gkv = room(RK)
        M8 = room(NB * 8).rearrange("p (j n) -> p j n", n=8)
        K8 = room(NB * 8).rearrange("p (j n) -> p j n", n=8)
        den = room(3 * NB).rearrange("p (a j) -> p a j", a=3)
        sq_junk = room(RQ)
        kv_junk = room(RK)
        zrow = room(R_W)
        assert at[0] <= B * HP * 2 * S

        WT = [KT[:, n, :].bitcast(F32)[:, 0:320] for n in range(2)]

        LR, SEL, EX, KEY = (x_sb.rearrange("p j n -> p (j n)")[:, i * NB * E:(i + 1) * NB * E]
                            .rearrange("p (j e) -> p j e", e=E) for i in range(4))
        ROPA, ROPB = (xnT[:, 0, i * NB * E:(i + 1) * NB * E].rearrange("p (j e) -> p j e", e=E) for i in range(2))
        KR = xnT[:, 1, :].rearrange("p (j n) -> p j n", n=P)
        dest = sb("destinations", [P, NB, 8], U32)

        work = sb("work", [P, 13840], F32)
        at[0] = 0

        def lot(n):
            a = work[:, at[0]:at[0] + n]
            at[0] += n
            return a

        WC0 = lot(2 * NH * P // 2).bitcast(F16).rearrange("p (l n) -> p l n", l=2)
        WC1 = lot(NH * P // 2).bitcast(F16)
        QA = lot(4 * T // 2).bitcast(F16).rearrange("p (k t) -> p k t", k=4)
        QR = [lot(512).rearrange("p (h n) -> p h n", h=4) for _ in range(2)]
        RT = [lot(256).rearrange("p (h n) -> p h n", h=4) for _ in range(2)]
        SELB, PREB = (QR[n].rearrange("p h n -> p (h n)").bitcast(BF16).rearrange("p (j e) -> p j e", e=E)
                      for n in range(2))
        rows_at = at[0]
        ROWS = lot(NB * R_W).rearrange("p (j n) -> p j n", n=R_W)
        at[0] = 0
        PR = [lot(2 * S).rearrange("p (s k) -> p s k", s=2) for _ in range(4)]
        PT = [lot(2 * S).rearrange("p (s k) -> p s k", s=2) for _ in range(2)]
        XB = [lot(R_W) for _ in range(2)]
        Y = [lot(H) for _ in range(2)]
        XBT = lot(H).rearrange("p (c n) -> p c n", c=NC)
        EG, D1, RG, GR, HM = (lot(F) for _ in range(5))
        HMT = lot(P)
        WCOL = [lot(1) for _ in range(2)]
        IDX = [lot(1).bitcast(U32) for _ in range(2)]
        assert at[0] <= rows_at
        at[0] = rows_at
        WGU = []
        WD = []
        for _ in range(4):
            WGU.append(lot(2 * 2 * NC * F).rearrange("p (e g n) -> p e g n", e=2, g=2))
            WD.append(lot(2 * H).rearrange("p (e n) -> p e n", e=2))
        at[0] = 0
        MA, MB, XR, OUT = ([lot(H) for _ in range(4)] for _ in range(4))

        nmax = small[:, 0:8].rearrange("p (g s) -> p g s", s=2)
        sums = small[:, 8:16].rearrange("p (g s) -> p g s", s=2)
        rinv = small[:, 16:24].rearrange("p (g s) -> p g s", s=2)

        bank = ctx.enter_context(nc.psum_tensor("psum", [P, 8, 512], F32))

        s_cst, s_wa, s_g, s_whead, s_wo = (sem(n) for n in ("s_cst", "s_wa", "s_g", "s_whead", "s_wo"))
        s_x = [sem(f"s_x{g}") for g in range(QB)]
        s_ones, s_zrow, s_init, s_moe0 = sem("s_ones"), sem("s_zrow"), sem("s_init"), sem("s_moe0")
        s_dv, s_dvr = sem("s_dve_step"), sem("s_dve_route")
        s_var, s_sd, s_xn, s_xt, s_xte = (sem(n) for n in ("s_var", "s_sd", "s_xn", "s_xt", "s_xte"))
        s_rt, s_rte, s_a, s_al, s_ssq = (sem(n) for n in ("s_rt", "s_rte", "s_a", "s_al", "s_ssq"))
        s_kss, s_rv, s_rsd, s_rr, s_qan = (sem(n) for n in ("s_kss", "s_rv", "s_rsd", "s_rr", "s_qan"))
        s_cb, s_wt, s_wte, s_cmb, s_vo = (sem(n) for n in ("s_cb", "s_wt", "s_wte", "s_cmb", "s_vo"))
        s_hic, s_loc, s_hivo, s_lovo, s_pehi, s_pelo = (
            sem(n) for n in ("s_hic", "s_loc", "s_hivo", "s_lovo", "s_pehi", "s_pelo"))
        s_warm = sem("s_warm")
        s_ropk, s_den, s_rowsw = sem("s_ropk"), sem("s_den"), sem("s_rowsw")
        s_v, s_kr, s_kt, s_khi, s_klo = (sem(n) for n in ("s_v", "s_kr", "s_kt", "s_khi", "s_klo"))
        s_qa, s_qahi, s_qalo = sem("s_qa"), sem("s_qahi"), sem("s_qalo")
        s_sub, s_ex, s_sel, s_pos, s_dest, s_rows, s_scat = (
            sem(n) for n in ("s_sub", "s_ex", "s_sel", "s_pos", "s_dest", "s_rows", "s_scat"))
        s_proj, s_ropa, s_rope, s_nope, s_qt, s_qhi, s_qlo = (
            sem(n) for n in ("s_proj", "s_ropa", "s_rope", "s_nope", "s_qt", "s_qhi", "s_qlo"))
        s_sc, s_max, s_exp, s_rin = (sem(n) for n in ("s_sc", "s_max", "s_exp", "s_rin"))
        s_nrm = [sem(f"s_nrm{s}") for s in range(2)]
        s_pt = [sem(f"s_pt{s}") for s in range(2)]
        s_pte = [sem(f"s_pte{s}") for s in range(2)]
        s_pv, s_ohi, s_olo = sem("s_pv"), sem("s_ohi"), sem("s_olo")
        s_w = [sem(f"s_w{q}") for q in range(4)]
        s_xb = [sem(f"s_xb{q}") for q in range(2)]
        s_f, s_xbt, s_eg, s_hd, s_hm, s_hmt, s_y, s_idx, s_add = (
            sem(n) for n in ("s_f", "s_xbt", "s_eg", "s_hd", "s_hm", "s_hmt", "s_y", "s_idx", "s_add"))
        s_base, s_bl, s_fin, s_o = sem("s_base"), [sem(f"s_bl{n}") for n in range(4)], sem("s_fin"), sem("s_o")
        s_out = [sem(f"s_out{n}") for n in range(4)]

        block = ctx.enter_context(nc.Block())

        def unit(u):
            return u // QB, IORDER[u % QB]

        def heads(a, n=NH):
            return a.rearrange("p (h n) -> p h n", h=n)

        def after(eng, semaphore, value):
            if not isinstance(value, int) or value > 0:
                eng.wait_ge(semaphore, value)

        def one(i):
            return bass.ds(i, 1)

        @block.sync
        def _(sp):
            sp.dma_start(cst[:, :], consts[:, 0:C_MASK]).then_inc(s_cst, 16)
            sp.dma_start(late_c, consts[:, C_MASK:C_W]).then_inc(s_cst, 16)
            for g in range(QB):
                sp.dma_start(x_sb[:, 4 * g:4 * g + 4, :], x_d[:, 4 * g:4 * g + 4, :]).then_inc(s_x[g], 16)
            sp.dma_start(WQ0.rearrange("p h n -> p (h n)"), w_q_b[0:P, :]).then_inc(s_whead, 16)
            sp.dma_start(WQ1.rearrange("p h n -> p (h n)")[0:RQ - P, :], w_q_b[P:RQ, :]).then_inc(s_whead, 16)
            sp.dma_start(WKV.rearrange("p h n -> p (h n)")[0:RK, :], w_kv_b).then_inc(s_whead, 16)
            sp.dma_start(WO, w_o.rearrange("(h v) n -> v h n", v=VD)).then_inc(s_wo, 16)
            sp.wait_ge(s_zrow, 2)
            sp.dma_start(slots_d.rearrange("(a p) n -> p a n", p=P),
                         zrow.unsqueeze(1).broadcast_to([P, SLOTS // P, R_W])).then_inc(s_init, 16)
            sp.dma_start(moe_d.rearrange("(a p) n -> p a n", p=P),
                         zrow[:, 0:H].unsqueeze(1).broadcast_to([P, 2 * MROWS // P, H])).then_inc(s_moe0, 16)

            def load_slots(q, p):
                k = q % 2
                sp.dma_start(XB[k], slots_d[bass.ds(p * P, P), :]).then_inc(s_xb[k], 16)
                for e in range(2):
                    sp.dma_start(WCOL[k][e * CAP:(e + 1) * CAP, :],
                                 slots_d[bass.ds(p * P + e * CAP, CAP), bass.ds(p * 2 + (R_WT + e), 1)],
                                 allow_slow_non_contiguous=True)\
                        .then_inc(s_xb[k], 16)

            def load_weights(q, p):
                for g, w in enumerate((w_gate, w_up)):
                    sp.dma_start(WGU[q][:, :, g, :],
                                 w[bass.ds(p * 2, 2), :, :].rearrange("e (p c) f -> p e (c f)", c=NC))\
                        .then_inc(s_w[q], 16)
                sp.dma_start(WD[q][0:F, :, :], w_down[bass.ds(p * 2, 2), :, :].rearrange("e f n -> f e n"))\
                    .then_inc(s_w[q], 16)

            sp.wait_ge(s_scat, 16 * NSC)
            sp.wait_ge(s_qt, 4 * NB)
            load_slots(0, 0)
            load_weights(0, 0)
            load_slots(1, 1)
            for q in range(1, 4):
                load_weights(q, q)

            def refill(hp, last):
                for q in range(4):
                    p = hp * 4 + q
                    if not last or q < 2:
                        sp.wait_ge(s_y, p + 1)
                        load_slots(q, p + 2)
                    if not last:
                        sp.wait_ge(s_f, p * 4 + 4)
                        load_weights(q, p + 4)

            refill(0, False)
            with sp.Fori(1, HP - 1) as hp:
                refill(hp, False)
            refill(HP - 1, True)

            sp.wait_ge(s_add, 16 * PAIRS)
            sp.wait_ge(s_pv, UNITS * HP)
            moe_v = [moe_d[a * MROWS:a * MROWS + T, :].rearrange("(j p) n -> p j n", p=P) for a in range(2)]

            def load_base(n, j):
                sp.dma_start(XR[n], x_d[:, one(j), :].rearrange("p a n -> p (a n)")).then_inc(s_bl[n], 16)
                for dst, a in ((MA, 0), (MB, 1)):
                    sp.dma_start(dst[n], moe_v[a][:, one(j), :].rearrange("p a n -> p (a n)")).then_inc(s_bl[n], 16)

            def store(n, j):
                sp.wait_ge(s_o, j + 1)
                sp.dma_start(out_d[:, one(j), :].rearrange("p a n -> p (a n)"), OUT[n]).then_inc(s_out[n], 16)

            for n in range(4):
                load_base(n, n)
            with sp.Fori(0, B - 1) as b:
                for n in range(4):
                    store(n, b * 4 + n)
                    load_base(n, b * 4 + n + 4)
            for n in range(4):
                store(n, (B - 1) * 4 + n)
            for n in range(4):
                sp.wait_ge(s_out[n], 16 * B)

        @block.gpsimd
        def _(pool):
            pool.memset(small[:, 40:41], 1.0).then_inc(s_warm, 1)
            pool.memset(onesb[:, :], 1.0).then_inc(s_ones, 1)
            pool.memset(zrow[:, 0:R_ID], 0.0).then_inc(s_zrow, 1)
            pool.wait_ge(s_rr, 1)
            for j in range(NB):
                pool.tensor_scalar(AL[:, j, 0:A_KV], AL[:, j, 0:A_KV], rr[:, 0, j:j + 1], 1.0, ALU.mult,
                                   ALU.mult).then_inc(s_qan, 1)
            kpe = AL[:, :, A_PE:A_RT].rearrange("p (b i) n -> p b i n", i=QB)
            cosk, sink = (cst[:, c:c + 256].rearrange("p (i n) -> p i n", i=QB).unsqueeze(1)
                          .broadcast_to([P, B, QB, ROPE]) for c in (C_COS, C_SIN))
            pool.wait_ge(s_a, NB)
            pool.tensor_tensor(ROPA.rearrange("p (b i) n -> p b i n", i=QB), kpe, cosk, ALU.mult).then_inc(s_ropk, 1)
            for n in range(2):
                o = 32 * n
                pool.tensor_tensor(ROPB.rearrange("p (b i) n -> p b i n", i=QB)[:, :, :, o:o + 32],
                                   kpe[:, :, :, 32 - o:64 - o], sink[:, :, :, o:o + 32], ALU.mult).then_inc(s_ropk, 1)
            pool.wait_ge(s_ropk, 3)
            pool.tensor_tensor(KR[:, :, RK:P], ROPA, ROPB, ALU.add).then_inc(s_kr, 1)
            pool.wait_ge(s_den, 1)
            pool.tensor_tensor(ROWS[:, :, R_WT:R_ID], EX, den[:, 0, :].unsqueeze(2).broadcast_to([P, NB, E]),
                               ALU.mult).then_inc(s_rowsw, 1)

            pool.wait_ge(s_init, 16)
            pool.wait_ge(s_dest, 1)
            pool.wait_ge(s_rows, 1)
            pool.wait_ge(s_rowsw, 1)
            for j in range(NB):
                for k in range(TOPK):
                    pool.indirect_dma_start(slots_d, bass.IndirectOffsetOnAxis(dest[:, j, k:k + 1], 0),
                                            ROWS[:, j, :], None, bounds_check=SLOTS - 1,
                                            oob_is_err=False).then_inc(s_scat, 16)
            pool.wait_ge(s_moe0, 16)

            def meet(cell):
                pool.tensor_tensor(small[0:1, 32 + cell:33 + cell], cst[0:1, 0:1], cst[0:1, 0:1], ALU.add)

            def norm(g, u):
                _, i = unit(u % UNITS)
                nk = (i + 1) * P
                pool.wait_ge(s_rin, g + 1)
                meet(u % 4)
                for s in range(2):
                    t = PR[u % 4][:, s, 0:nk]
                    pool.tensor_scalar(t, t, rinv[:, u % 4, s:s + 1], 1.0, ALU.mult, ALU.mult).then_inc(s_nrm[s], 1)

            def add_rows(q, p):
                pool.wait_ge(s_y, p + 1)
                pool.wait_ge(s_idx, p + 1)
                after(pool, s_add, p * 16)
                meet(4 + q)
                pool.indirect_dma_start(moe_d, bass.IndirectOffsetOnAxis(IDX[q % 2], 0), Y[q % 2], None,
                                        bounds_check=2 * MROWS - 1, compute_op=ALU.add).then_inc(s_add, 16)

            for u in range(2):
                norm(u, u)

            def step(hp, last):
                for u in range(UNITS):
                    g = hp * UNITS + u
                    if not last or u + 2 < UNITS:
                        norm(g + 2, u + 2)
                    if u % 4 == 3:
                        add_rows(u // 4, hp * 4 + u // 4)

            step(0, False)
            with pool.Fori(1, HP - 1) as hp:
                step(hp, False)
            step(HP - 1, True)

            def base(n, b):
                pool.wait_ge(s_bl[n], b * 48 + 48)
                pool.tensor_tensor(XR[n], XR[n], MA[n], ALU.add).then_inc(s_base, 1)
                pool.wait_ge(s_base, (b * 4 + n) * 2 + 1)
                pool.tensor_tensor(XR[n], XR[n], MB[n], ALU.add).then_inc(s_base, 1)

            with pool.Fori(0, B) as b:
                for n in range(4):
                    base(n, b)

        @block.scalar
        def _(act):
            act.dma_start(rt_row[0:E, :], router_w).then_inc(s_wa, 16)
            wqa = w_q_a.rearrange("(c p) n -> p c n", p=P)
            act.dma_start(WA[:, :, 0:RQ], wqa).then_inc(s_wa, 16)
            act.dma_start(WA[:, :, A_DUP:A_KV], wqa[:, :, P:RQ]).then_inc(s_wa, 16)
            act.dma_start(WA[:, :, A_KV:A_RT], w_kv_a.rearrange("(c p) n -> p c n", p=P)).then_inc(s_wa, 16)
            act.wait_ge(s_warm, 1)
            act.activation(small[:, 40:41], small[:, 40:41], ACT.Sqrt)
            act.dma_start(gq[:, 0:1], g_q_a[0:P].unsqueeze(1)).then_inc(s_g, 16)
            act.dma_start(gq[0:RQ - P, 1:2], g_q_a[P:RQ].unsqueeze(1)).then_inc(s_g, 16)
            act.dma_start(gkv, g_kv_a.unsqueeze(0).broadcast_to([P, RK])).then_inc(s_g, 16)

            for g in range(QB):
                act.wait_ge(s_var, g + 1)
                act.activation(sd[:, 4 * g:4 * g + 4], ve[:, 4 * g:4 * g + 4], ACT.Sqrt).then_inc(s_sd, 1)
            act.wait_ge(s_rt, 1)
            act.wait_ge(s_wa, 64)
            act.activation(WA[:, :, A_RT:A_W], bank[:, 2, 0:2 * E].rearrange("p (c e) -> p c e", c=NC), ACT.Copy)\
                .then_inc(s_rte, 1)

            def xt_out(g):
                for c in range(NC):
                    act.wait_ge(s_xt, g * NC + c + 1)
                    act.activation(xnT[:, c, g * S:(g + 1) * S], bank[:, c, :], ACT.Copy).then_inc(s_xte, 1)

            def first_out(j):
                act.wait_ge(s_a, j + 1)
                act.activation(AL[:, j, :], bank[:, 2 + j % 2, 0:A_W], ACT.Copy).then_inc(s_al, 1)
                act.wait_ge(s_al, j + 1)
                if j >= 1:
                    act.wait_ge(s_ssq, j)
                act.activation(sq_junk, AL[:, j, 0:RQ], ACT.Square, accum_out=ssq[:, 0, j:j + 1]).then_inc(s_ssq, 1)

            xt_out(0)
            for g in range(QB):
                if g + 1 < QB:
                    xt_out(g + 1)
                for n in range(4):
                    first_out(4 * g + n)
            act.wait_ge(s_rv, 2)
            act.activation(rsd, rv, ACT.Sqrt).then_inc(s_rsd, 1)
            act.wait_ge(s_sub, 1)
            act.activation(EX, EX, ACT.Exp).then_inc(s_ex, 1)

            act.wait_ge(s_cb, 5)
            act.wait_ge(s_whead, 48)
            act.activation(heads(WC0[:, 0, :])[:, :, 64:P], WQ0[:, :, NOPE:RQ], ACT.Copy,
                           scale=gs[:, 0:1]).then_inc(s_pehi, 1)
            act.activation(heads(WC1)[0:64, :, 64:P], WQ1[0:64, :, NOPE:RQ], ACT.Copy,
                           scale=gs[0:64, 1:2]).then_inc(s_pehi, 1)
            for hd in range(NH + 1):
                if hd < NH:
                    act.wait_ge(s_wt, hd + 1)
                    if hd >= 2:
                        act.wait_ge(s_vo, hd - 1)
                    act.activation(WT[hd % 2], bank[:, 4 + hd % 2, 0:320], ACT.Copy).then_inc(s_wte, 1)
                if hd >= 2 and hd % 2 == 0:
                    act.wait_ge(s_vo, hd)
                    n = hd // 2 - 1
                    act.activation(WVO[:, 0, n, :], bank[:, (2 + n) % 4, 0:H], ACT.Copy).then_inc(s_hivo, 1)
                if hd >= 8 and hd % 8 == 0:
                    n = hd // 8 - 1
                    act.wait_ge(s_cmb, n + 1)
                    act.activation(heads(WC0[:, 0, :])[:, 8 * n:8 * n + 8, 0:64], heads(bank[:, 6, :], 8), ACT.Copy,
                                   scale=gs[:, 0:1]).then_inc(s_hic, 1)
                    act.activation(heads(WC1)[0:64, 8 * n:8 * n + 8, 0:64], heads(bank[0:64, 7, :], 8), ACT.Copy,
                                   scale=gs[0:64, 1:2]).then_inc(s_hic, 1)

            act.wait_ge(s_v, 1)
            act.activation(KR[:, :, 0:RK], V[:, :, :], ACT.Copy).then_inc(s_kr, 1)
            for g in range(QB):
                act.wait_ge(s_kt, g + 1)
                act.activation(KT[:, 0, g * S:(g + 1) * S], bank[:, g % 2, :], ACT.Copy).then_inc(s_khi, 1)
            for g in range(QB):
                for c in range(2):
                    n = 2 * g + c
                    act.wait_ge(s_qa, n + 1)
                    act.activation(QA[:, 2 * c, g * S:(g + 1) * S], bank[:, 2 + n % 2, :], ACT.Copy).then_inc(s_qahi, 1)

            def nope(g, m):
                act.wait_ge(s_ropa, g + 1)
                act.activation(QR[m % 2][:, :, 0:64], bank[:, m % 4, :].rearrange("p (h n) -> p h n", h=4)[:, :, 0:64],
                               ACT.Copy).then_inc(s_nope, 1)

            def q_high(g, b, m):
                act.wait_ge(s_qt, g + 1)
                n, cols = m % 4, slice((m // 4) * P, (m // 4 + 1) * P)
                act.activation(Q[:, one(b), 2 * n:2 * n + 2, :, 0, cols].rearrange("p a h s q -> p (a h s) q"),
                               bank[:, 4 + n, :].rearrange("p (h q) -> p h q", h=4), ACT.Copy).then_inc(s_qhi, 1)

            def queries(b, last):
                for m in range(16):
                    g = b * 16 + m
                    if not last or m + 1 < 16:
                        nope(g + 1, m + 1)
                    q_high(g, b, m)

            act.wait_ge(s_moe0, 16)
            act.wait_ge(s_rowsw, 1)
            nope(0, 0)
            queries(0, False)
            with act.Fori(1, B - 1) as b:
                queries(b, False)
            queries(B - 1, True)

            def exps(g, u):
                _, i = unit(u % UNITS)
                nk = (i + 1) * P
                act.wait_ge(s_max, g + 1)
                for s in range(2):
                    ins = act.activation(PR[u % 4][:, s, 0:nk], bank[:, 2 * (u % 2) + s, 0:nk], ACT.Exp,
                                         bias=nmax[:, u % 4, s:s + 1], accum_out=sums[:, u % 4, s:s + 1])
                ins.then_inc(s_exp, 1)

            def pt_out(g, u):
                _, i = unit(u % UNITS)
                nk = (i + 1) * P
                act.wait_ge(s_pt[1], g + 1)
                act.activation(PT[u % 2][:, 1, 0:nk], bank[:, 5, 0:nk], ACT.Copy).then_inc(s_pte[1], 1)

            def o_high(g, hp, u):
                b, i = unit(u)
                act.wait_ge(s_pv, g + 1)
                act.activation(Q[:, b, one(hp), 0, 0, i * P:(i + 1) * P].rearrange("p a q -> p (a q)"),
                               bank[:, 6, 0:P], ACT.Copy).then_inc(s_ohi, 1)

            def experts(g, hp, u):
                q, f = u // 4, u % 4
                p = hp * 4 + q
                if f == 0:
                    act.wait_ge(s_f, g + 1)
                    act.activation(XBT.rearrange("p c n -> p (c n)"), bank[:, 7, 0:H], ACT.Copy).then_inc(s_xbt, 1)
                if f == 1:
                    act.wait_ge(s_f, g + 1)
                    act.activation(EG, bank[:, 7, 0:F], ACT.Exp, scale=-1.0).then_inc(s_eg, 1)
                if f == 2:
                    act.wait_ge(s_f, g + 1)
                    act.activation(HMT[0:F, :], bank[0:F, 7, 0:P], ACT.Copy).then_inc(s_hmt, 1)

            act.wait_ge(s_qt, 4 * NB)
            for u in range(2):
                exps(u, u)
            pt_out(0, 0)

            def attend(hp, last):
                for u in range(UNITS):
                    g = hp * UNITS + u
                    if u > 0:
                        o_high(g - 1, hp, u - 1)
                    experts(g, hp, u)
                    if not last or u + 2 < UNITS:
                        exps(g + 2, u + 2)
                    if not last or u + 1 < UNITS:
                        pt_out(g + 1, u + 1)
                o_high(hp * UNITS + UNITS - 1, hp, UNITS - 1)

            attend(0, False)
            with act.Fori(1, HP - 1) as hp:
                attend(hp, False)
            attend(HP - 1, True)

        @block.vector
        def _(dve):
            step = [0]

            def link(ins):
                step[0] += 1
                ins.then_inc(s_dv, 1)
                dve.wait_ge(s_dv, step[0])

            dve.wait_ge(s_cst, 32)
            dve.tensor_copy(identb[:, :], ident).then_inc(s_cb, 1)
            dve.tensor_copy(maskb[:, :], late_c[:, 0:P]).then_inc(s_cb, 1)
            dve.tensor_copy(trib[:, :], late_c[:, P:2 * P]).then_inc(s_cb, 1)
            dve.tensor_copy(zrow[:, R_ID:R_W], cst[:, C_DEF:C_DEF + 1]).then_inc(s_zrow, 1)

            for g in range(QB):
                dve.wait_ge(s_x[g], 16)
                for j in range(4 * g, 4 * g + 4):
                    ins = dve.bn_stats(bn6[:, j, :], x_sb[:, j, :])
                link(ins)
                for j in range(4 * g, 4 * g + 4):
                    ins = dve.bn_aggr(mv[:, j, :], bn6[:, j, :])
                link(ins)
                dve.tensor_scalar(ve[:, 4 * g:4 * g + 4], mv[:, 4 * g:4 * g + 4, 1], LN_EPS, None, ALU.add)\
                    .then_inc(s_var, 1)

            def rsqrt(y, root, v, t):
                link(dve.reciprocal(y, root))
                link(dve.tensor_tensor(t, y, y, ALU.mult))
                link(dve.tensor_tensor(t, t, v, ALU.mult))
                link(dve.tensor_scalar(t, t, -0.5, 1.5, ALU.mult, ALU.add))
                return dve.tensor_tensor(y, y, t, ALU.mult)

            for g in range(QB):
                dve.wait_ge(s_sd, g + 1)
                a = slice(4 * g, 4 * g + 4)
                link(rsqrt(rs[:, a], sd[:, a], ve[:, a], nt[:, a]))
                for j in range(4 * g, 4 * g + 4):
                    ins = dve.tensor_scalar(ROWS[:, j, 0:H], x_sb[:, j, :], mv[:, j, 0:1], rs[:, j:j + 1],
                                            ALU.subtract, ALU.mult)
                ins.then_inc(s_xn, 1)
            dve.tensor_copy(ROWS[:, :, R_ID:R_W], cst[:, C_TOK:C_TOK + NB].unsqueeze(2)).then_inc(s_rows, 1)
            dve.wait_ge(s_g, 48)
            dve.tensor_scalar(gs[:, 0:1], gq[:, 0:1], SCALE, None, ALU.mult).then_inc(s_cb, 1)
            dve.tensor_scalar(gs[0:64, 1:2], gq[0:64, 1:2], SCALE, None, ALU.mult).then_inc(s_cb, 1)

            for j in range(NB):
                dve.wait_ge(s_al, j + 1)
                dve.max(M8[:, j, :], AL[:, j, A_RT:A_W])
                ins = dve.tensor_tensor_reduce(out=kv_junk, in0=AL[:, j, A_KV:A_PE], in1=AL[:, j, A_KV:A_PE],
                                               scale=1.0, scalar=0.0, op0=ALU.mult, op1=ALU.add,
                                               accum_out=ssq[:, 1, j:j + 1])
                link(ins)
            dve.wait_ge(s_ssq, NB)
            dve.tensor_scalar(rv[:, 0, :], ssq[:, 0, :], 1.0 / RQ, RMS_EPS, ALU.mult, ALU.add).then_inc(s_rv, 1)
            dve.tensor_scalar(rv[:, 1, :], ssq[:, 1, :], 1.0 / RK, RMS_EPS, ALU.mult, ALU.add).then_inc(s_rv, 1)

            for j in range(NB):
                ins = dve.match_replace(LR[:, j, :], M8[:, j, :], AL[:, j, A_RT:A_W], -3e38)
            link(ins)
            logits = AL[:, :, A_RT:A_W]
            link(dve.tensor_tensor(SEL, LR, logits, ALU.not_equal))
            dve.tensor_copy(SELB, SEL)
            link(dve.memset(PREB[:, 0, :], 0.0))
            for j in range(1, NB - 1):
                link(dve.tensor_tensor(PREB[:, j, :], PREB[:, j - 1, :], SELB[:, j - 1, :], ALU.add))
            dve.tensor_tensor(PREB[:, NB - 1, :], PREB[:, NB - 2, :], SELB[:, NB - 2, :], ALU.add).then_inc(s_sel, 1)
            dve.tensor_tensor(EX, logits, M8[:, :, 0:1].broadcast_to([P, NB, E]), ALU.subtract).then_inc(s_sub, 1)

            dve.wait_ge(s_rsd, 1)
            rsqrt(rr, rsd, rv, rt).then_inc(s_rr, 1)
            dve.wait_ge(s_rr, 1)
            for j in range(NB):
                ins = dve.scalar_tensor_tensor(out=V[:, j, :], in0=AL[:, j, A_KV:A_PE], scalar=rr[:, 1, j:j + 1],
                                               in1=gkv, op0=ALU.mult, op1=ALU.mult)
            ins.then_inc(s_v, 1)

            dve.wait_ge(s_pos, 1)
            for n in range(2):
                a = slice(8 * n, 8 * n + 8)
                pos = heads(bank[:, n, :], 8)
                dve.scalar_tensor_tensor(out=LR[:, a, :], in0=pos, scalar=float(CAP), in1=SEL[:, a, :],
                                         op0=ALU.is_lt, op1=ALU.mult)
                ins = dve.tensor_tensor(KEY[:, a, :], cst[:, C_KEY:C_KEY + E].unsqueeze(1).broadcast_to([P, 8, E]), pos,
                                        ALU.subtract)
            link(ins)
            link(dve.tensor_tensor(KEY, KEY, LR, ALU.mult))
            for j in range(NB):
                ins = dve.max(K8[:, j, :], KEY[:, j, :])
            link(ins)
            dve.tensor_scalar(dest[:, :, :], K8, -1.0, float(SLOTS), ALU.mult, ALU.add).then_inc(s_dest, 1)

            dve.wait_ge(s_ex, 1)
            link(dve.tensor_reduce(den[:, 0, :], EX, AX.X, ALU.add))
            link(dve.tensor_tensor(EX, EX, SEL, ALU.mult))
            link(dve.tensor_reduce(den[:, 1, :], EX, AX.X, ALU.add))
            link(dve.scalar_tensor_tensor(out=den[:, 2, :], in0=den[:, 0, :], scalar=1e-20, in1=den[:, 1, :],
                                          op0=ALU.mult, op1=ALU.add))
            dve.reciprocal(den[:, 0, :], den[:, 2, :]).then_inc(s_den, 1)

            def low_scaled(dst, src, scale, high):
                return dve.scalar_tensor_tensor(out=dst, in0=src, scalar=scale, in1=high, op0=ALU.mult,
                                                op1=ALU.subtract)

            dve.wait_ge(s_pehi, 2)
            low_scaled(heads(WC0[:, 1, :])[:, :, 64:P], WQ0[:, :, NOPE:RQ], gs[:, 0:1],
                       heads(WC0[:, 0, :])[:, :, 64:P]).then_inc(s_pelo, 1)
            low_scaled(heads(WC1)[64:P, :, 64:P], WQ1[0:64, :, NOPE:RQ], gs[0:64, 1:2],
                       heads(WC1)[0:64, :, 64:P]).then_inc(s_pelo, 1)
            for n in range(HP):
                dve.wait_ge(s_hivo, n + 1)
                dve.tensor_tensor(WVO[:, 1, n, :], bank[:, (2 + n) % 4, 0:H], WVO[:, 0, n, :], ALU.subtract)\
                    .then_inc(s_lovo, 1)
                if n % 4 == 3:
                    m = n // 4
                    a = slice(8 * m, 8 * m + 8)
                    dve.wait_ge(s_hic, 2 * m + 2)
                    low_scaled(heads(WC0[:, 1, :])[:, a, 0:64], heads(bank[:, 6, :], 8), gs[:, 0:1],
                               heads(WC0[:, 0, :])[:, a, 0:64]).then_inc(s_loc, 1)
                    low_scaled(heads(WC1)[64:P, a, 0:64], heads(bank[0:64, 7, :], 8), gs[0:64, 1:2],
                               heads(WC1)[0:64, a, 0:64]).then_inc(s_loc, 1)

            for g in range(QB):
                dve.wait_ge(s_khi, g + 1)
                cols = slice(g * S, (g + 1) * S)
                dve.tensor_tensor(KT[:, 1, cols], bank[:, g % 2, :], KT[:, 0, cols], ALU.subtract).then_inc(s_klo, 1)
            for g in range(QB):
                for c in range(2):
                    n = 2 * g + c
                    dve.wait_ge(s_qahi, n + 1)
                    cols = slice(g * S, (g + 1) * S)
                    dve.tensor_tensor(QA[:, 2 * c + 1, cols], bank[:, 2 + n % 2, :], QA[:, 2 * c, cols],
                                      ALU.subtract).then_inc(s_qalo, 1)

            def rotate(g, m):
                i = (m // 4) % QB
                pe = heads(bank[:, m % 4, :], 4)[:, :, 64:P]
                qr, tmp = QR[m % 2], RT[m % 2]
                cos, sin = (cst[:, c + i * 64:c + (i + 1) * 64].unsqueeze(1).broadcast_to([P, 4, ROPE])
                            for c in (C_COS, C_SIN))
                halves = "p h (a n) -> p h a n"
                dve.wait_ge(s_proj, g + 1)
                after(dve, s_qt, g - 1)
                dve.tensor_tensor(qr[:, :, 64:P], pe, cos, ALU.mult)
                dve.tensor_tensor(tmp.rearrange(halves, a=2), pe.rearrange(halves, a=2)[:, :, ::-1, :],
                                  sin.rearrange(halves, a=2), ALU.mult).then_inc(s_ropa, 1)
                dve.wait_ge(s_ropa, g + 1)
                dve.tensor_tensor(qr[:, :, 64:P], qr[:, :, 64:P], tmp, ALU.add).then_inc(s_rope, 1)

            def q_low(g, b, m):
                dve.wait_ge(s_qhi, g + 1)
                n, cols = m % 4, slice((m // 4) * P, (m // 4 + 1) * P)
                q = [Q[:, one(b), 2 * n:2 * n + 2, :, l, cols].rearrange("p a h s q -> p (a h s) q") for l in range(2)]
                dve.tensor_tensor(q[1], heads(bank[:, 4 + n, :], 4), q[0], ALU.subtract).then_inc(s_qlo, 1)

            def queries(b, last):
                for m in range(16):
                    g = b * 16 + m
                    if not last or m + 1 < 16:
                        rotate(g + 1, m + 1)
                    if m > 0:
                        q_low(g - 1, b, m - 1)
                q_low(b * 16 + 15, b, 15)

            rotate(0, 0)
            queries(0, False)
            with dve.Fori(1, B - 1) as b:
                queries(b, False)
            queries(B - 1, True)

            def row_max(g, u):
                _, i = unit(u % UNITS)
                dve.wait_ge(s_sc, g + 1)
                x = 2 * (u % 2)
                dve.tensor_reduce(nmax[:, u % 4, :], bank[:, x:x + 2, 0:(i + 1) * P], AX.X, ALU.max, negate=True)\
                    .then_inc(s_max, 1)

            def recip(g, u):
                dve.wait_ge(s_exp, g + 1)
                dve.reciprocal(rinv[:, u % 4, :], sums[:, u % 4, :]).then_inc(s_rin, 1)

            def pt_out(g, u):
                _, i = unit(u % UNITS)
                nk = (i + 1) * P
                dve.wait_ge(s_pt[0], g + 1)
                dve.tensor_copy(PT[u % 2][:, 0, 0:nk], bank[:, 4, 0:nk]).then_inc(s_pte[0], 1)

            def o_low(g, hp, u):
                b, i = unit(u)
                dve.wait_ge(s_ohi, g + 1)
                o = [Q[:, b, one(hp), 0, l, i * P:(i + 1) * P].rearrange("p a q -> p (a q)") for l in range(2)]
                dve.tensor_tensor(o[1], bank[:, 6, 0:P], o[0], ALU.subtract).then_inc(s_olo, 1)

            def experts(g, hp, u):
                q, f = u // 4, u % 4
                p = hp * 4 + q
                if f == 0:
                    after(dve, s_add, p * 16 - 16)
                    dve.wait_ge(s_xb[q % 2], (hp * 2 + q // 2) * 48 + 48)
                    dve.tensor_tensor(IDX[q % 2], XB[q % 2][:, R_ID:R_W], cst[:, C_OFF:C_OFF + 1], ALU.add)\
                        .then_inc(s_idx, 1)
                if f == 1:
                    dve.wait_ge(s_eg, p + 1)
                    dve.tensor_scalar(D1, EG, 1.0, None, ALU.add).then_inc(s_hd, 1)
                    dve.wait_ge(s_hd, p * 3 + 1)
                    dve.reciprocal(RG, D1).then_inc(s_hd, 1)
                    dve.wait_ge(s_hd, p * 3 + 2)
                    dve.tensor_tensor(GR, bank[:, 7, 0:F], RG, ALU.mult).then_inc(s_hd, 1)
                    dve.wait_ge(s_hd, p * 3 + 3)
                    dve.tensor_tensor(HM, bank[:, 7, F:2 * F], GR, ALU.mult).then_inc(s_hm, 1)
                if f == 3:
                    dve.wait_ge(s_f, g + 1)
                    dve.tensor_scalar(Y[q % 2], bank[:, 7, 0:H], WCOL[q % 2], None, ALU.mult).then_inc(s_y, 1)

            for u in range(3):
                row_max(u, u)
                if u < 2:
                    recip(u, u)
            pt_out(0, 0)

            def attend(hp, last):
                for u in range(UNITS):
                    g = hp * UNITS + u
                    if u > 0:
                        o_low(g - 1, hp, u - 1)
                    experts(g, hp, u)
                    if not last or u + 3 < UNITS:
                        row_max(g + 3, u + 3)
                    if not last or u + 2 < UNITS:
                        recip(g + 2, u + 2)
                    if not last or u + 1 < UNITS:
                        pt_out(g + 1, u + 1)
                o_low(hp * UNITS + UNITS - 1, hp, UNITS - 1)

            attend(0, False)
            with dve.Fori(1, HP - 1) as hp:
                attend(hp, False)
            attend(HP - 1, True)

            def finish(b, n):
                j = b * 4 + n
                dve.wait_ge(s_fin, j + 1)
                dve.wait_ge(s_base, j * 2 + 2)
                after(dve, s_out[n], b * 16)
                dve.tensor_tensor(OUT[n], bank[:, n, 0:H], XR[n], ALU.add).then_inc(s_o, 1)

            for n in range(4):
                finish(0, n)
            with dve.Fori(1, B) as b:
                for n in range(4):
                    finish(b, n)

        @block.tensor
        def _(pe):
            pe.wait_ge(s_cst, 32)
            pe.wait_ge(s_wa, 64)
            for c in range(NC):
                ins = pe.transpose(bank[:, 2, c * E:(c + 1) * E], rt_row[0:E, c * P:(c + 1) * P], ident[0:E, 0:E])
            ins.then_inc(s_rt, 1)

            def x_t(g):
                pe.wait_ge(s_xn, g + 1)
                for c in range(NC):
                    if g >= 1:
                        pe.wait_ge(s_xte, (g - 1) * NC + c + 1)
                    for n in range(4):
                        ins = pe.transpose(bank[:, c, n * P:(n + 1) * P], ROWS[:, 4 * g + n, c * P:(c + 1) * P], ident)
                    ins.then_inc(s_xt, 1)

            def first(j):
                pe.wait_ge(s_xte, (j // 4 + 1) * NC)
                if j >= 2:
                    pe.wait_ge(s_al, j - 1)
                for c in range(NC):
                    ins = pe.matmul(bank[:, 2 + j % 2, 0:A_W], xnT[:, c, j * P:(j + 1) * P], WA[:, c, :],
                                    start=(c == 0), stop=(c == NC - 1))
                ins.then_inc(s_a, 1)

            x_t(0)
            pe.wait_ge(s_rte, 1)
            for g in range(QB):
                if g + 1 < QB:
                    x_t(g + 1)
                for n in range(4):
                    first(4 * g + n)

            pe.wait_ge(s_cb, 3)
            pe.wait_ge(s_ones, 1)
            pe.wait_ge(s_sel, 1)
            for n in range(2):
                a = slice(8 * n, 8 * n + 8)
                pe.matmul(bank[:, n, :], trib[:, :], SELB[:, a, :].rearrange("p j e -> p (j e)"), start=True, stop=False)
                ins = pe.matmul(bank[:, n, :], onesb[:, :], PREB[:, a, :].rearrange("p j e -> p (j e)"), start=False,
                                stop=True)
            ins.then_inc(s_pos, 1)

            pe.wait_ge(s_whead, 48)
            pe.wait_ge(s_wo, 16)

            def head_t(hd):
                if hd >= 2:
                    pe.wait_ge(s_wte, hd - 1)
                o = bank[:, 4 + hd % 2, :]
                pe.transpose(o[:, 0:P], WQ0[:, hd, 0:NOPE], ident)
                pe.transpose(o[:, P:RQ], WQ1[0:64, hd, 0:NOPE], ident[0:64, 0:64])
                pe.transpose(o[:, RQ:256], WKV[0:64, hd, 0:NOPE], ident[0:64, 0:64])
                pe.transpose(o[:, 256:320], WKV[0:64, hd, NOPE:256], ident[0:64, 0:64]).then_inc(s_wt, 1)

            def head_products(hd):
                pe.wait_ge(s_wte, hd + 1)
                w, n, k = WT[hd % 2], hd // 2, hd % 8
                if hd == 8:
                    pe.wait_ge(s_loc, 2)
                pe.matmul(bank[:, 6, k * 64:(k + 1) * 64], w[:, 0:P], w[:, RQ:256], start=True, stop=True)
                ins = pe.matmul(bank[0:64, 7, k * 64:(k + 1) * 64], w[:, P:RQ], w[:, RQ:256], start=True, stop=True)
                if k == 7:
                    ins.then_inc(s_cmb, 1)
                if hd == 0:
                    pe.wait_ge(s_al, NB)
                if hd == 4:
                    pe.wait_ge(s_dest, 1)
                if n >= 4 and hd % 2 == 0:
                    pe.wait_ge(s_lovo, n - 3)
                r = 64 * (hd % 2)
                pe.matmul(bank[r:r + 64, (2 + n) % 4, 0:H], w[:, 256:320], WO[:, hd, :], start=True, stop=True)\
                    .then_inc(s_vo, 1)

            head_t(0)
            for hd in range(NH):
                if hd + 1 < NH:
                    head_t(hd + 1)
                head_products(hd)

            pe.wait_ge(s_kr, 2)
            pe.wait_ge(s_lovo, HP)
            for g in range(QB):
                if g >= 2:
                    pe.wait_ge(s_klo, g - 1)
                for n in range(4):
                    ins = pe.transpose(bank[:, g % 2, n * P:(n + 1) * P], KR[:, 4 * g + n, :], ident)
                ins.then_inc(s_kt, 1)
            pe.wait_ge(s_qan, NB)
            for g in range(QB):
                for c in range(2):
                    m = 2 * g + c
                    if m >= 2:
                        pe.wait_ge(s_qalo, m - 1)
                    for n in range(4):
                        a0 = 0 if c == 0 else P
                        ins = pe.transpose(bank[:, 2 + m % 2, n * P:(n + 1) * P], AL[:, 4 * g + n, a0:a0 + P], ident)
                    ins.then_inc(s_qa, 1)

            def project(g, b, m):
                j = b * 4 + m // 4
                n = m % 4
                after(pe, s_nope, g - 3)
                w = [WC0[:, 0, n * S:(n + 1) * S], WC0[:, 1, n * S:(n + 1) * S], WC1[:, n * S:(n + 1) * S]]
                for k, (a, c) in enumerate(((0, 0), (0, 1), (1, 0), (2, 2), (3, 2))):
                    x = QA[:, a, bass.ds(j * P, P)]
                    ins = pe.matmul(bank[:, n, :], x, w[c], start=(k == 0), stop=(k == 4))
                ins.then_inc(s_proj, 1)

            def q_t(g, m):
                pe.wait_ge(s_rope, g + 1)
                pe.wait_ge(s_nope, g + 1)
                after(pe, s_qlo, g - 3)
                for k in range(4):
                    ins = pe.transpose(bank[:, 4 + m % 4, k * P:(k + 1) * P], QR[m % 2][:, k, :], ident)
                ins.then_inc(s_qt, 1)

            def queries(b, last):
                for m in range(16):
                    g = b * 16 + m
                    if not last or m + 2 < 16:
                        project(g + 2, b if m + 2 < 16 else b + 1, (m + 2) % 16)
                    q_t(g, m)

            pe.wait_ge(s_klo, QB)
            pe.wait_ge(s_qalo, 2 * QB)
            pe.wait_ge(s_loc, 4)
            pe.wait_ge(s_pelo, 2)
            project(0, 0, 0)
            project(1, 0, 1)
            queries(0, False)
            with pe.Fori(1, B - 1) as b:
                queries(b, False)
            queries(B - 1, True)

            def scores(g, hp, u):
                b, i = unit(u)
                nk = (i + 1) * P
                after(pe, s_exp, g - 1)
                for s in range(2):
                    o = bank[:, 2 * (u % 2) + s, :]
                    q = [Q[:, b, one(hp), s, l, i * P:nk].rearrange("p a q -> p (a q)") for l in range(2)]
                    k = [KT[:, l, b * S:b * S + nk] for l in range(2)]
                    pe.matmul(o[:, 0:nk], q[0], k[0], start=True, stop=False)
                    pe.matmul(o[:, 0:nk], q[0], k[1], start=False, stop=False)
                    pe.matmul(o[:, 0:nk], q[1], k[0], start=False, stop=False)
                    ins = pe.matmul(o[:, i * P:nk], identb[:, :], maskb[:, :], start=False, stop=True)
                ins.then_inc(s_sc, 1)

            def probs_t(g, u):
                _, i = unit(u)
                for s in range(2):
                    pe.wait_ge(s_nrm[s], g + 1)
                    after(pe, s_pte[s], g)
                    for k in range(i + 1):
                        ins = pe.transpose(bank[:, 4 + s, k * P:(k + 1) * P], PR[u % 4][:, s, k * P:(k + 1) * P], ident)
                    ins.then_inc(s_pt[s], 1)

            def values(g, u):
                b, i = unit(u)
                for s in range(2):
                    pe.wait_ge(s_pte[s], g + 1)
                after(pe, s_olo, g)
                for k in range(i + 1):
                    for s in range(2):
                        ins = pe.matmul(bank[64 * s:64 * s + 64, 6, 0:P], V[:, b * QB + k, :],
                                        PT[u % 2][:, s, k * P:(k + 1) * P], start=(k == 0), stop=(k == i))
                ins.then_inc(s_pv, 1)

            def experts(g, hp, u):
                q, f = u // 4, u % 4
                p = hp * 4 + q
                if f == 0:
                    pe.wait_ge(s_xb[q % 2], (hp * 2 + q // 2) * 48 + 48)
                    after(pe, s_y, p)
                    for c in range(NC):
                        ins = pe.transpose(bank[:, 7, c * P:(c + 1) * P], XB[q % 2][:, c:H:NC], ident)
                if f == 1:
                    pe.wait_ge(s_xbt, p + 1)
                    pe.wait_ge(s_w[q], hp * 48 + 48)
                    for c in range(NC):
                        for e in range(2):
                            r = 64 * e
                            ins = pe.matmul(bank[r:r + 64, 7, 0:2 * F].rearrange("p (g n) -> p g n", g=2),
                                            XBT[:, c, r:r + 64], WGU[q][:, e, :, c * F:(c + 1) * F],
                                            start=(c == 0), stop=(c == NC - 1))
                if f == 2:
                    pe.wait_ge(s_hm, p + 1)
                    ins = pe.transpose(bank[0:F, 7, 0:P], HM, ident)
                if f == 3:
                    pe.wait_ge(s_hmt, p + 1)
                    for e in range(2):
                        r = 64 * e
                        ins = pe.matmul(bank[r:r + 64, 7, 0:H], HMT[0:F, r:r + 64], WD[q][0:F, e, :], start=True,
                                        stop=True)
                ins.then_inc(s_f, 1)

            pe.wait_ge(s_nope, 4 * NB)
            pe.wait_ge(s_qlo, 4 * NB)
            for u in range(3):
                scores(u, 0, u)
            probs_t(0, 0)

            def attend(hp, last):
                for u in range(UNITS):
                    g = hp * UNITS + u
                    experts(g, hp, u)
                    if not last or u + 3 < UNITS:
                        scores(g + 3, hp if u + 3 < UNITS else hp + 1, (u + 3) % UNITS)
                    if not last or u + 1 < UNITS:
                        probs_t(g + 1, (u + 1) % UNITS)
                    values(g, u)

            attend(0, False)
            with pe.Fori(1, HP - 1) as hp:
                attend(hp, False)
            attend(HP - 1, True)

            def project_out(b, n):
                after(pe, s_o, b * 4 + n - 3)
                for hp in range(HP):
                    o = [Q[:, one(b), hp, 0, l, n * P:(n + 1) * P].rearrange("p a q -> p (a q)") for l in range(2)]
                    for k, (x, w) in enumerate(((0, 0), (0, 1), (1, 0))):
                        ins = pe.matmul(bank[:, n, 0:H], o[x], WVO[:, w, hp, :], start=(hp == 0 and k == 0),
                                        stop=(hp == HP - 1 and k == 2))
                ins.then_inc(s_fin, 1)

            pe.wait_ge(s_exp, UNITS * HP)
            pe.wait_ge(s_olo, UNITS * HP)
            for n in range(4):
                project_out(0, n)
            with pe.Fori(1, B) as b:
                for n in range(4):
                    project_out(b, n)


_INS = ['L0_attn_h', 'L0_attn_w_q_a', 'L0_attn_g_q_a', 'L0_attn_w_q_b', 'L0_attn_w_kv_a', 'L0_attn_g_kv_a',
        'L0_attn_w_kv_b', 'L0_attn_w_o', 'L0_ffn_router_w', 'L0_ffn_w_gate', 'L0_ffn_w_up', 'L0_ffn_w_down']
_OUTS = [((B, S, H), 'float32')]


def kernel(**inputs):
    import numpy as _np
    import concourse.bacc as _bacc
    from concourse import mybir as _mybir
    from concourse.bass_utils import run_bass_kernel_spmd as _run

    nc = _bacc.Bacc("TRN2", target_bir_lowering=False, num_devices=1)
    arrays, args = {}, []
    for name in _INS:
        a = _np.ascontiguousarray(inputs[name])
        arrays[f"in_{name}_dram"] = a
        args.append(nc.dram_tensor(f"in_{name}_dram", a.shape, _mybir.dt.from_np(a.dtype), kind="ExternalInput").ap())
    arrays["constants_dram"] = table()
    args.append(nc.dram_tensor("constants_dram", (P, C_W), F32, kind="ExternalInput").ap())
    for i, (shape, dtype) in enumerate(_OUTS):
        dt = _mybir.dt.from_np(_np.dtype(dtype))
        args.append(nc.dram_tensor(f"out_{i}_dram", shape, dt, kind="ExternalOutput").ap())
    mla_moe_kernel(nc, *args)
    r = _run(nc, [arrays], core_ids=[0])
    got = tuple(r.results[0][f"out_{i}_dram"] for i in range(len(_OUTS)))
    return got[0]
```

```python
from contextlib import ExitStack

import concourse.bass as bass
from concourse import mybir

ALU = mybir.AluOpType
ACT = mybir.ActivationFunctionType
AX = mybir.AxisListType
F32 = mybir.dt.float32
F16 = mybir.dt.float16
BF16 = mybir.dt.bfloat16
U32 = mybir.dt.uint32

P = 128
B, S, H = 4, 512, 256
T = B * S
NH, NOPE, ROPE, VD = 16, 128, 64, 128
RQ, RK = 192, 64
E, TOPK, F, CAP = 64, 8, 96, 64
NB = T // P
QB = S // P
HP = NH // 2
NC = H // P
SCALE = float((NOPE + ROPE) ** -0.5)
LN_EPS, RMS_EPS = 1e-5, 1e-6

W_KV, W_RT, W_W = RQ, RQ + RK + ROPE, RQ + RK + ROPE + E
A_DUP, A_KV, A_PE, A_RT, A_W = RQ, RQ + 64, RQ + 64 + RK, RQ + 64 + RK + ROPE, RQ + 64 + RK + ROPE + E

R_WT, R_W = H, H + E
MROWS = T + CAP

C_COS, C_SIN, C_ID, C_KEY, C_OFF, C_SLOT, C_MASK, C_W = 0, 256, 512, 640, 656, 658, 659, 787

IORDER = [3, 2, 1, 0]
UNITS = B * QB
DVE_NORM = (0,)
PAIRS = E // 2
ROUNDS = 9


def table():
    import numpy as np

    c = np.zeros((P, C_W), np.float32)
    pos = np.arange(S, dtype=np.float32)
    inv = (1.0 / np.float32(10000.0) ** (np.arange(0, ROPE, 2, dtype=np.float32) / np.float32(ROPE))).astype(np.float32)
    ang = (pos[:, None] * inv[None, :]).astype(np.float32)
    cos, sin = np.cos(ang).astype(np.float32), np.sin(ang).astype(np.float32)
    for i in range(QB):
        rows = slice(i * P, (i + 1) * P)
        c[:, C_COS + i * 64:C_COS + (i + 1) * 64] = np.concatenate([cos[rows], cos[rows]], 1)
        c[:, C_SIN + i * 64:C_SIN + (i + 1) * 64] = np.concatenate([-sin[rows], sin[rows]], 1)
    p = np.arange(P)
    c[:, C_ID:C_ID + P] = np.eye(P)
    c[:, C_KEY:C_KEY + NB] = T - (p[:, None] + P * np.arange(NB)[None, :])
    c[:, C_OFF + 1] = np.where(p < CAP, 0, MROWS)
    c[:, C_SLOT] = p % CAP
    c[:, C_MASK:C_MASK + P] = np.where(p[None, :] > p[:, None], -1e30, 0.0)
    return c


def mla_moe_kernel(nc, h, w_q_a, g_q_a, w_q_b, w_kv_a, g_kv_a, w_kv_b, w_o, router_w, w_gate, w_up,
                   w_down, consts, out):
    x_d = h.rearrange("b (i p) n -> p (b i) n", p=P)
    out_d = out.rearrange("b (i p) n -> p (b i) n", p=P)
    rows_d = nc.dram_tensor("token_rows", [T + CAP, R_W], F32, kind="Internal").ap()
    first_d = nc.dram_tensor("first_tokens", [E, CAP], F32, kind="Internal").ap()
    moe_d = nc.dram_tensor("moe_sums", [2 * MROWS, H], F32, kind="Internal").ap()

    with ExitStack() as ctx:
        def sb(name, shape, dt):
            return ctx.enter_context(nc.sbuf_tensor(name, shape, dt))

        def sem(name):
            return ctx.enter_context(nc.semaphore(name))

        qreg = sb("queries", [P, B * HP * 2 * 2 * S], F16)
        Q = qreg[:, :].rearrange("p (b h s l q) -> p b h s l q", b=B, h=HP, s=2, l=2)
        KT = sb("keys_t", [P, 2, T], F16)
        V = sb("values", [P, NB, RK], F32)
        WVO = sb("w_values_out", [P, 2, HP, H], F16)
        cst = sb("constants", [P, C_MASK], F32)
        ident = cst[:, C_ID:C_ID + P]
        identb = sb("identity_bf16", [P, P], BF16)
        maskb = sb("causal_mask", [P, P], BF16)
        KM = sb("first_of_halves", [P, 8 * ROUNDS + CAP], F32)
        EIGHT = sb("eight_keys", [P, 8], F32)
        K64 = sb("first_of_all", [E, CAP], F32)
        KX = sb("first_by_slot", [P, PAIRS], F32)
        ROWNO = sb("slot_rows", [P, PAIRS], F32)
        EMPTY = sb("slot_empty", [P, PAIRS], F32)
        small = sb("small", [P, 64], F32)

        early = qreg[:, :].bitcast(F32)
        at = [0]

        def room(n):
            a = early[:, at[0]:at[0] + n]
            at[0] += n
            return a

        xnT = room(NC * T).rearrange("p (c t) -> p c t", c=NC)
        x_sb = room(NB * H).rearrange("p (j n) -> p j n", n=H)
        WQ0 = room(NH * RQ).rearrange("p (h n) -> p h n", h=NH)
        WQ1 = room(NH * RQ).rearrange("p (h n) -> p h n", h=NH)
        WKV = room(NH * 256).rearrange("p (h n) -> p h n", h=NH)
        WO = room(NH * H).rearrange("p (h n) -> p h n", h=NH)
        AL = room(NB * A_W).rearrange("p (j n) -> p j n", n=A_W)
        wa_at = at[0]
        WA = room(NC * W_W).rearrange("p (c n) -> p c n", c=NC)
        rt_row = room(H)
        late_c = room(P)
        bn6 = room(NB * 6).rearrange("p (j n) -> p j n", n=6)
        mv = room(NB * 2).rearrange("p (j n) -> p j n", n=2)
        ve, sd, rs, nt = (room(NB) for _ in range(4))
        ssq, rv, rsd, rr, rt = (room(2 * NB).rearrange("p (a j) -> p a j", a=2) for _ in range(5))
        gq = room(2)
        gs = room(2)
        gkv = room(RK)
        M8 = room(NB * 8).rearrange("p (j n) -> p j n", n=8)
        den = room(3 * NB).rearrange("p (a j) -> p a j", a=3)
        sq_junk = room(RQ)
        kv_junk = room(RK)
        zrow = room(R_W)
        assert at[0] <= B * HP * 2 * S

        WT = [KT[:, n, :].bitcast(F32)[:, 0:320] for n in range(2)]

        LR, SEL, EX = (x_sb.rearrange("p j n -> p (j n)")[:, i * NB * E:(i + 1) * NB * E]
                            .rearrange("p (j e) -> p j e", e=E) for i in range(3))
        SELK = LR.rearrange("p (j a) e -> p j a e", a=2)
        assert wa_at + NC * W_W + H >= wa_at + T // 2 and wa_at >= 3 * HP * 2 * S
        KEYT = early[:, wa_at:wa_at + T // 2]
        assert TOPK == 8 and CAP % 8 == 0 and 8 * ROUNDS >= CAP
        ROPA, ROPB = (xnT[:, 0, i * NB * E:(i + 1) * NB * E].rearrange("p (j e) -> p j e", e=E) for i in range(2))
        KR = xnT[:, 1, :].rearrange("p (j n) -> p j n", n=P)

        work = sb("work", [P, 13824], F32)
        xb0 = sb("expert_rows0", [P, R_W], F32)
        wcol = sb("slot_weights", [P, 2], F32)
        WCOL = [wcol[:, n:n + 1] for n in range(2)]
        idx = sb("indices", [P, 8], U32)
        at[0] = 0

        def lot(n):
            a = work[:, at[0]:at[0] + n]
            at[0] += n
            return a

        WC0 = lot(2 * NH * P // 2).bitcast(F16).rearrange("p (l n) -> p l n", l=2)
        WC1 = lot(NH * P // 2).bitcast(F16)
        QA = lot(4 * T // 2).bitcast(F16).rearrange("p (k t) -> p k t", k=4)
        QR = [lot(512).rearrange("p (h n) -> p h n", h=4) for _ in range(2)]
        RT = [lot(256).rearrange("p (h n) -> p h n", h=4) for _ in range(2)]
        rows_at = at[0]
        ROWS = lot(NB * R_W).rearrange("p (j n) -> p j n", n=R_W)
        at[0] = 0
        PR = [lot(2 * S).rearrange("p (s k) -> p s k", s=2) for _ in range(4)]
        PT = [lot(2 * S).rearrange("p (s k) -> p s k", s=2) for _ in range(2)]
        XB = [xb0[:, :], lot(R_W)]
        Y = [lot(H) for _ in range(2)]
        XBT = lot(H).rearrange("p (c n) -> p c n", c=NC)
        EG, D1, RG, GR, HM = (lot(F) for _ in range(5))
        HMT = lot(P)
        assert at[0] <= rows_at
        at[0] = rows_at
        QR += [work[:, rows_at + 3840 + 512 * n:rows_at + 4352 + 512 * n].rearrange("p (h n) -> p h n", h=4)
               for n in range(2)]
        RT += [work[:, rows_at + 3328 + 256 * n:rows_at + 3584 + 256 * n].rearrange("p (h n) -> p h n", h=4)
               for n in range(2)]
        WGU = []
        WD = []
        for _ in range(4):
            WGU.append(lot(2 * 2 * NC * F).rearrange("p (e g n) -> p e g n", e=2, g=2))
            WD.append(lot(2 * H).rearrange("p (e n) -> p e n", e=2))
        at[0] = 0
        MA, MB, XR, OUT = ([lot(H) for _ in range(4)] for _ in range(4))

        nmax = small[:, 0:8].rearrange("p (g s) -> p g s", s=2)
        sums = small[:, 8:16].rearrange("p (g s) -> p g s", s=2)
        rinv = small[:, 16:24].rearrange("p (g s) -> p g s", s=2)

        bank = ctx.enter_context(nc.psum_tensor("psum", [P, 8, 512], F32))

        s_cst, s_wa, s_g, s_whead, s_wo = (sem(n) for n in ("s_cst", "s_wa", "s_g", "s_whead", "s_wo"))
        s_x = [sem(f"s_x{g}") for g in range(QB)]
        s_zrow, s_rowsd, s_moe0 = sem("s_zrow"), sem("s_rowsd"), sem("s_moe0")
        s_dv = sem("s_dve_step")
        s_var, s_sd, s_xn, s_xt, s_xte = (sem(n) for n in ("s_var", "s_sd", "s_xn", "s_xt", "s_xte"))
        s_rt, s_rte, s_a, s_al, s_ssq = (sem(n) for n in ("s_rt", "s_rte", "s_a", "s_al", "s_ssq"))
        s_rv, s_rsd, s_rr, s_qan = (sem(n) for n in ("s_rv", "s_rsd", "s_rr", "s_qan"))
        s_cb, s_wt, s_wte, s_cmb, s_vo = (sem(n) for n in ("s_cb", "s_wt", "s_wte", "s_cmb", "s_vo"))
        s_hic, s_loc, s_hivo, s_lovo, s_pehi, s_pelo = (
            sem(n) for n in ("s_hic", "s_loc", "s_hivo", "s_lovo", "s_pehi", "s_pelo"))
        s_warm = sem("s_warm")
        s_ropk, s_den, s_rowsw = sem("s_ropk"), sem("s_den"), sem("s_rowsw")
        s_v, s_kr, s_kt, s_khi, s_klo = (sem(n) for n in ("s_v", "s_kr", "s_kt", "s_khi", "s_klo"))
        s_qa, s_qahi, s_qalo = sem("s_qa"), sem("s_qahi"), sem("s_qalo")
        s_sub, s_ex, s_sel, s_selk, s_selt, s_key = (
            sem(n) for n in ("s_sub", "s_ex", "s_sel", "s_selk", "s_selt", "s_key"))
        s_tk, s_first, s_firstd, s_kx, s_no = (sem(n) for n in ("s_tk", "s_first", "s_firstd", "s_kx", "s_no"))
        s_proj, s_ropa, s_cos, s_rope, s_nope, s_qt, s_qhi, s_qlo = (
            sem(n) for n in ("s_proj", "s_ropa", "s_cos", "s_rope", "s_nope", "s_qt", "s_qhi", "s_qlo"))
        s_sc, s_max, s_exp, s_rin = (sem(n) for n in ("s_sc", "s_max", "s_exp", "s_rin"))
        s_nrm = [sem(f"s_nrm{s}") for s in range(2)]
        s_nrmv = sem("s_nrmv")
        s_pt = [sem(f"s_pt{s}") for s in range(2)]
        s_pte = [sem(f"s_pte{s}") for s in range(2)]
        s_pv, s_ohi, s_olo = sem("s_pv"), sem("s_ohi"), sem("s_olo")
        s_w = [sem(f"s_w{q}") for q in range(4)]
        s_xb = [sem(f"s_xb{q}") for q in range(2)]
        s_wc = [sem(f"s_wc{q}") for q in range(2)]
        s_f, s_xbt, s_eg, s_hd, s_hm, s_hmt, s_y, s_add = (
            sem(n) for n in ("s_f", "s_xbt", "s_eg", "s_hd", "s_hm", "s_hmt", "s_y", "s_add"))
        s_base, s_bl, s_fin, s_o = sem("s_base"), [sem(f"s_bl{n}") for n in range(4)], sem("s_fin"), sem("s_o")
        s_out = [sem(f"s_out{n}") for n in range(4)]

        block = ctx.enter_context(nc.Block())

        def unit(u):
            return u // QB, IORDER[u % QB]

        def heads(a, n=NH):
            return a.rearrange("p (h n) -> p h n", h=n)

        def after(eng, semaphore, value):
            if not isinstance(value, int) or value > 0:
                eng.wait_ge(semaphore, value)

        def one(i):
            return bass.ds(i, 1)

        @block.sync
        def _(sp):
            for g in range(QB):
                sp.dma_start(x_sb[:, 4 * g:4 * g + 4, :], x_d[:, 4 * g:4 * g + 4, :]).then_inc(s_x[g], 16)
                if g == 0:
                    sp.dma_start(cst[:, :], consts[:, 0:C_MASK]).then_inc(s_cst, 16)
                    sp.dma_start(late_c, consts[:, C_MASK:C_W]).then_inc(s_cst, 16)
            sp.dma_start(WQ0.rearrange("p h n -> p (h n)"), w_q_b[0:P, :]).then_inc(s_whead, 16)
            sp.dma_start(WQ1.rearrange("p h n -> p (h n)")[0:RQ - P, :], w_q_b[P:RQ, :]).then_inc(s_whead, 16)
            sp.dma_start(WKV.rearrange("p h n -> p (h n)")[0:RK, :], w_kv_b).then_inc(s_whead, 16)
            sp.dma_start(WO, w_o.rearrange("(h v) n -> v h n", v=VD)).then_inc(s_wo, 16)
            sp.wait_ge(s_zrow, 1)
            sp.dma_start(rows_d[T:T + CAP, :], zrow[0:CAP, :]).then_inc(s_rowsd, 16)
            sp.dma_start(moe_d.rearrange("(a p) n -> p a n", p=P),
                         zrow[:, 0:H].unsqueeze(1).broadcast_to([P, 2 * MROWS // P, H])).then_inc(s_moe0, 16)

            rows_v = rows_d[0:T, :].rearrange("(j p) n -> p j n", p=P)
            sp.wait_ge(s_xn, QB)
            sp.dma_start(rows_v[:, :, 0:H], ROWS[:, :, 0:H]).then_inc(s_rowsd, 16)
            sp.wait_ge(s_rowsw, 1)
            sp.dma_start(rows_v[:, :, R_WT:R_W], ROWS[:, :, R_WT:R_W]).then_inc(s_rowsd, 16)

            def slot_weights(k, n, p):
                sp.wait_ge(s_xb[k], n * 16)
                for e in range(2):
                    r = slice(e * CAP, (e + 1) * CAP)
                    sp.dma_start(WCOL[k][r, :], XB[k][r, bass.ds(p * 2 + (R_WT + e), 1)],
                                 allow_slow_non_contiguous=True).then_inc(s_wc[k], 16)

            def load_weights(q, p):
                for g, w in enumerate((w_gate, w_up)):
                    sp.dma_start(WGU[q][:, :, g, :],
                                 w[bass.ds(p * 2, 2), :, :].rearrange("e (p c) f -> p e (c f)", c=NC))\
                        .then_inc(s_w[q], 16)
                sp.dma_start(WD[q][0:F, :, :], w_down[bass.ds(p * 2, 2), :, :].rearrange("e f n -> f e n"))\
                    .then_inc(s_w[q], 16)

            sp.wait_ge(s_rowsd, 48)
            for q in range(2):
                load_weights(q, q)
            sp.wait_ge(s_first, 8)
            sp.dma_start(first_d, K64[:, :]).then_inc(s_firstd, 16)
            sp.wait_ge(s_firstd, 16)
            for e in range(2):
                sp.dma_start(KX[e * CAP:(e + 1) * CAP, :], first_d.rearrange("(a e) c -> e c a", e=2)[e],
                             allow_slow_non_contiguous=True).then_inc(s_kx, 16)
            slot_weights(0, 1, 0)
            sp.wait_ge(s_qt, 4 * NB)
            for q in range(2, 4):
                load_weights(q, q)
            slot_weights(1, 1, 1)

            def refill(hp, last):
                for q in range(4):
                    p = hp * 4 + q
                    if not last or q < 2:
                        sp.wait_ge(s_y, p + 1)
                        slot_weights(q % 2, hp * 2 + q // 2 + 2, p + 2)
                    if not last:
                        sp.wait_ge(s_f, p * 4 + 4)
                        load_weights(q, p + 4)

            refill(0, False)
            with sp.Fori(1, HP - 1) as hp:
                refill(hp, False)
            refill(HP - 1, True)

            sp.wait_ge(s_add, 16 * PAIRS)
            sp.wait_ge(s_pv, UNITS * HP)
            moe_v = [moe_d[a * MROWS:a * MROWS + T, :].rearrange("(j p) n -> p j n", p=P) for a in range(2)]

            def load_base(n, j):
                sp.dma_start(XR[n], x_d[:, one(j), :].rearrange("p a n -> p (a n)")).then_inc(s_bl[n], 16)
                for dst, a in ((MA, 0), (MB, 1)):
                    sp.dma_start(dst[n], moe_v[a][:, one(j), :].rearrange("p a n -> p (a n)")).then_inc(s_bl[n], 16)

            def store(n, j):
                sp.wait_ge(s_o, j + 1)
                sp.dma_start(out_d[:, one(j), :].rearrange("p a n -> p (a n)"), OUT[n]).then_inc(s_out[n], 16)

            for n in range(4):
                load_base(n, n)
            with sp.Fori(0, B - 1) as b:
                for n in range(4):
                    store(n, b * 4 + n)
                    load_base(n, b * 4 + n + 4)
            for n in range(4):
                store(n, (B - 1) * 4 + n)
            for n in range(4):
                sp.wait_ge(s_out[n], 16 * B)

        @block.gpsimd
        def _(pool):
            pool.memset(small[:, 40:41], 1.0).then_inc(s_warm, 1)
            pool.memset(zrow, 0.0).then_inc(s_zrow, 1)
            kpe = AL[:, :, A_PE:A_RT].rearrange("p (b i) n -> p b i n", i=QB)
            cosk, sink = (cst[:, c:c + 256].rearrange("p (i n) -> p i n", i=QB).unsqueeze(1)
                          .broadcast_to([P, B, QB, ROPE]) for c in (C_COS, C_SIN))
            pool.wait_ge(s_al, NB)
            pool.tensor_tensor(ROPA.rearrange("p (b i) n -> p b i n", i=QB), kpe, cosk, ALU.mult).then_inc(s_ropk, 1)
            for n in range(2):
                o = 32 * n
                pool.tensor_tensor(ROPB.rearrange("p (b i) n -> p b i n", i=QB)[:, :, :, o:o + 32],
                                   kpe[:, :, :, 32 - o:64 - o], sink[:, :, :, o:o + 32], ALU.mult).then_inc(s_ropk, 1)
            pool.wait_ge(s_ropk, 3)
            pool.tensor_tensor(KR[:, :, RK:P], ROPA, ROPB, ALU.add).then_inc(s_kr, 1)
            pool.wait_ge(s_rr, 1)
            for j in range(NB):
                pool.tensor_scalar(AL[:, j, 0:A_KV], AL[:, j, 0:A_KV], rr[:, 0, j:j + 1], 1.0, ALU.mult,
                                   ALU.mult).then_inc(s_qan, 1)
            pool.wait_ge(s_sel, 1)
            for n in range(2):
                a = slice(8 * n, 8 * n + 8)
                pool.tensor_tensor(SELK[:, :, n, :], SEL[:, a, :], cst[:, C_KEY + 8 * n:C_KEY + 8 * n + 8].unsqueeze(2)
                                   .broadcast_to([P, 8, E]), ALU.mult).then_inc(s_selk, 1)
            pool.wait_ge(s_den, 1)
            pool.tensor_tensor(ROWS[:, :, R_WT:R_W], EX, den[:, 0, :].unsqueeze(2).broadcast_to([P, NB, E]),
                               ALU.mult).then_inc(s_rowsw, 1)

            def meet(cell):
                pool.tensor_tensor(small[0:1, 32 + cell:33 + cell], cst[0:1, 0:1], cst[0:1, 0:1], ALU.add)

            def fetch(q, p):
                pool.wait_ge(s_no, p + 1)
                after(pool, s_y, p - 1)
                meet(8 + q)
                pool.indirect_dma_start(XB[q % 2], None, rows_d,
                                        bass.IndirectOffsetOnAxis(idx[:, 2 * q:2 * q + 1], 0),
                                        bounds_check=T + CAP - 1).then_inc(s_xb[q % 2], 16)

            def norm(g, u):
                _, i = unit(u % UNITS)
                nk = (i + 1) * P
                pool.wait_ge(s_rin, g + 1)
                meet(u % 4)
                for s in range(1 if i in DVE_NORM else 2):
                    t = PR[u % 4][:, s, 0:nk]
                    pool.tensor_scalar(t, t, rinv[:, u % 4, s:s + 1], 1.0, ALU.mult, ALU.mult).then_inc(s_nrm[s], 1)

            def add_rows(q, p):
                pool.wait_ge(s_y, p + 1)
                after(pool, s_add, p * 16)
                meet(4 + q)
                pool.indirect_dma_start(moe_d, bass.IndirectOffsetOnAxis(idx[:, 2 * q + 1:2 * q + 2], 0), Y[q % 2], None,
                                        bounds_check=2 * MROWS - 1, compute_op=ALU.add).then_inc(s_add, 16)

            def rope(g, m):
                i = (m // 4) % QB
                qr = QR[m % 4][:, :, 64:P]
                pool.wait_ge(s_nope, g + 1)
                cos = cst[:, C_COS + i * 64:C_COS + (i + 1) * 64].unsqueeze(1).broadcast_to([P, 4, ROPE])
                pool.tensor_tensor(qr, qr, cos, ALU.mult).then_inc(s_cos, 1)
                pool.wait_ge(s_cos, g + 1)
                pool.tensor_tensor(qr, qr, RT[m % 4], ALU.add).then_inc(s_rope, 1)

            with pool.Fori(0, B - 1) as b:
                for m in range(16):
                    rope(b * 16 + m, m)
            for m in range(16):
                if m == 15:
                    pool.wait_ge(s_rowsd, 48)
                    fetch(0, 0)
                rope((B - 1) * 16 + m, m)
            for u in range(2):
                norm(u, u)
            pool.wait_ge(s_qt, 4 * NB)
            fetch(1, 1)
            pool.wait_ge(s_moe0, 16)

            def step(hp, last):
                for u in range(UNITS):
                    g = hp * UNITS + u
                    q = u // 4
                    if not last or u + 2 < UNITS:
                        norm(g + 2, u + 2)
                    if u % 4 == 0 and not (last and q == 3) and not (isinstance(hp, int) and hp == 0 and q == 0):
                        fetch((q + 1) % 4, hp * 4 + q + 1)
                    if u % 4 == 3:
                        add_rows(u // 4, hp * 4 + u // 4)

            step(0, False)
            with pool.Fori(1, HP - 1) as hp:
                step(hp, False)
            step(HP - 1, True)

            def base(n, b):
                pool.wait_ge(s_bl[n], b * 48 + 48)
                pool.tensor_tensor(XR[n], XR[n], MA[n], ALU.add).then_inc(s_base, 1)
                pool.wait_ge(s_base, (b * 4 + n) * 2 + 1)
                pool.tensor_tensor(XR[n], XR[n], MB[n], ALU.add).then_inc(s_base, 1)

            with pool.Fori(0, B) as b:
                for n in range(4):
                    base(n, b)

        @block.scalar
        def _(act):
            act.dma_start(rt_row[0:E, :], router_w).then_inc(s_wa, 16)
            wqa = w_q_a.rearrange("(c p) n -> p c n", p=P)
            act.dma_start(WA[:, :, 0:RQ], wqa).then_inc(s_wa, 16)
            act.dma_start(WA[:, :, W_KV:W_RT], w_kv_a.rearrange("(c p) n -> p c n", p=P)).then_inc(s_wa, 16)
            act.wait_ge(s_warm, 1)
            act.activation(small[:, 40:41], small[:, 40:41], ACT.Sqrt)
            act.dma_start(gq[:, 0:1], g_q_a[0:P].unsqueeze(1)).then_inc(s_g, 16)
            act.dma_start(gq[0:RQ - P, 1:2], g_q_a[P:RQ].unsqueeze(1)).then_inc(s_g, 16)
            act.dma_start(gkv, g_kv_a.unsqueeze(0).broadcast_to([P, RK])).then_inc(s_g, 16)

            def root(g):
                act.wait_ge(s_var, g + 1)
                act.activation(sd[:, 4 * g:4 * g + 4], ve[:, 4 * g:4 * g + 4], ACT.Sqrt).then_inc(s_sd, 1)

            root(0)
            act.wait_ge(s_rt, 1)
            act.wait_ge(s_wa, 48)
            act.activation(WA[:, :, W_RT:W_W], bank[:, 2, 0:2 * E].rearrange("p (c e) -> p c e", c=NC), ACT.Copy)\
                .then_inc(s_rte, 1)

            def xt_out(g):
                for c in range(NC):
                    act.wait_ge(s_xt, g * NC + c + 1)
                    act.activation(xnT[:, c, g * S:(g + 1) * S], bank[:, c, :], ACT.Copy).then_inc(s_xte, 1)

            def first_out(j):
                act.wait_ge(s_a, j + 1)
                act.activation(AL[:, j, 0:RQ], bank[:, 2 + j % 2, 0:RQ], ACT.Copy)
                act.activation(AL[:, j, A_DUP:A_W], bank[:, 2 + j % 2, P:W_W], ACT.Copy).then_inc(s_al, 1)
                act.wait_ge(s_al, j + 1)
                if j >= 1:
                    act.wait_ge(s_ssq, j)
                act.activation(sq_junk, AL[:, j, 0:RQ], ACT.Square, accum_out=ssq[:, 0, j:j + 1]).then_inc(s_ssq, 1)

            root(1)
            xt_out(0)
            for g in range(QB):
                for n in range(4):
                    if n == 2 and g + 2 < QB:
                        root(g + 2)
                    if n == 2 and g + 1 < QB:
                        xt_out(g + 1)
                    first_out(4 * g + n)
            act.wait_ge(s_rv, 2)
            act.activation(rsd, rv, ACT.Sqrt).then_inc(s_rsd, 1)

            act.wait_ge(s_cb, 4)
            for hd in range(NH + 1):
                if hd < NH:
                    act.wait_ge(s_wt, hd + 1)
                    if hd >= 2:
                        act.wait_ge(s_vo, hd - 1)
                    act.activation(WT[hd % 2], bank[:, 4 + hd % 2, 0:320], ACT.Copy).then_inc(s_wte, 1)
                if hd >= 2 and hd % 2 == 0:
                    act.wait_ge(s_vo, hd)
                    n = hd // 2 - 1
                    act.activation(WVO[:, 0, n, :], bank[:, n % 2, 0:H], ACT.Copy).then_inc(s_hivo, 1)
                if hd == 14:
                    act.wait_ge(s_whead, 48)
                    act.activation(heads(WC0[:, 0, :])[:, :, 64:P], WQ0[:, :, NOPE:RQ], ACT.Copy,
                                   scale=gs[:, 0:1]).then_inc(s_pehi, 1)
                    act.activation(heads(WC1)[0:64, :, 64:P], WQ1[0:64, :, NOPE:RQ], ACT.Copy,
                                   scale=gs[0:64, 1:2]).then_inc(s_pehi, 1)
                if hd == 6:
                    act.wait_ge(s_v, 1)
                    act.activation(KR[:, :, 0:RK], V[:, :, :], ACT.Copy).then_inc(s_kr, 1)
                if hd == 9:
                    act.wait_ge(s_sub, 1)
                    act.activation(EX, EX, ACT.Exp).then_inc(s_ex, 1)
                if hd >= 8 and hd % 8 == 0:
                    n = hd // 8 - 1
                    act.wait_ge(s_cmb, n + 1)
                    act.activation(heads(WC0[:, 0, :])[:, 8 * n:8 * n + 8, 0:64], heads(bank[:, 6 - 4 * n, :], 8), ACT.Copy,
                                   scale=gs[:, 0:1]).then_inc(s_hic, 1)
                    act.activation(heads(WC1)[0:64, 8 * n:8 * n + 8, 0:64], heads(bank[0:64, 7 - 4 * n, :], 8), ACT.Copy,
                                   scale=gs[0:64, 1:2]).then_inc(s_hic, 1)

            for g in range(QB):
                act.wait_ge(s_kt, g + 1)
                act.activation(KT[:, 0, g * S:(g + 1) * S], bank[:, 4 + g, :], ACT.Copy).then_inc(s_khi, 1)
            for m in range(2 * QB):
                g, c = m // 2, m % 2
                act.wait_ge(s_qa, m + 1)
                act.activation(QA[:, 2 * c, g * S:(g + 1) * S], bank[:, 4 + m % 4, :], ACT.Copy).then_inc(s_qahi, 1)
                if m == 1:
                    act.wait_ge(s_selt, 1)
                    act.activation(KEYT, bank[:, 2:4, :].rearrange("p a n -> p (a n)"), ACT.Copy).then_inc(s_key, 1)

            def four_heads(g, m):
                act.wait_ge(s_ropa, g + 1)
                after(act, s_qt, g - 3)
                act.activation(QR[m % 4].rearrange("p h n -> p (h n)"), bank[:, m % 4, :], ACT.Copy).then_inc(s_nope, 1)

            def q_high(g, b, m):
                act.wait_ge(s_qt, g + 1)
                n, cols = m % 4, slice((m // 4) * P, (m // 4 + 1) * P)
                act.activation(Q[:, one(b), 2 * n:2 * n + 2, :, 0, cols].rearrange("p a h s q -> p (a h s) q"),
                               bank[:, 4 + n, :].rearrange("p (h q) -> p h q", h=4), ACT.Copy).then_inc(s_qhi, 1)

            def queries(b, last):
                for m in range(16):
                    g = b * 16 + m
                    if not last or m + 2 < 16:
                        four_heads(g + 2, m + 2)
                    if last and m == 15:
                        act.wait_ge(s_proj, 4 * NB)
                        exps(0, 0)
                    q_high(g, b, m)


            def exps(g, u):
                _, i = unit(u % UNITS)
                nk = (i + 1) * P
                act.wait_ge(s_max, g + 1)
                for s in range(2):
                    ins = act.activation(PR[u % 4][:, s, 0:nk], bank[:, 2 * (u % 2) + s, 0:nk], ACT.Exp,
                                         bias=nmax[:, u % 4, s:s + 1], accum_out=sums[:, u % 4, s:s + 1])
                ins.then_inc(s_exp, 1)

            def pt_out(g, u):
                _, i = unit(u % UNITS)
                nk = (i + 1) * P
                act.wait_ge(s_pt[1], g + 1)
                act.activation(PT[u % 2][:, 1, 0:nk], bank[:, 5, 0:nk], ACT.Copy).then_inc(s_pte[1], 1)

            def o_high(g, hp, u):
                b, i = unit(u)
                act.wait_ge(s_pv, g + 1)
                act.activation(Q[:, b, one(hp), 0, 0, i * P:(i + 1) * P].rearrange("p a q -> p (a q)"),
                               bank[:, 6, 0:P], ACT.Copy).then_inc(s_ohi, 1)

            def experts(g, hp, u):
                q, f = u // 4, u % 4
                p = hp * 4 + q
                if f == 0:
                    act.wait_ge(s_f, g + 1)
                    act.activation(XBT.rearrange("p c n -> p (c n)"), bank[:, 7, 0:H], ACT.Copy).then_inc(s_xbt, 1)
                if f == 1:
                    act.wait_ge(s_f, g + 1)
                    act.activation(EG, bank[:, 7, 0:F], ACT.Exp, scale=-1.0).then_inc(s_eg, 1)
                if f == 2:
                    act.wait_ge(s_f, g + 1)
                    act.activation(HMT[0:F, :], bank[0:F, 7, 0:P], ACT.Copy).then_inc(s_hmt, 1)

            act.wait_ge(s_moe0, 16)
            act.wait_ge(s_rowsw, 1)
            four_heads(0, 0)
            four_heads(1, 1)
            queries(0, False)
            with act.Fori(1, B - 1) as b:
                queries(b, False)
            act.wait_ge(s_tk, 3 * ROUNDS)
            queries(B - 1, True)

            exps(1, 1)
            act.wait_ge(s_qt, 4 * NB)
            pt_out(0, 0)

            def attend(hp, last):
                for u in range(UNITS):
                    g = hp * UNITS + u
                    if u > 0:
                        o_high(g - 1, hp, u - 1)
                    experts(g, hp, u)
                    if not last or u + 2 < UNITS:
                        exps(g + 2, u + 2)
                    if not last or u + 1 < UNITS:
                        pt_out(g + 1, u + 1)
                o_high(hp * UNITS + UNITS - 1, hp, UNITS - 1)

            attend(0, False)
            with act.Fori(1, HP - 1) as hp:
                attend(hp, False)
            attend(HP - 1, True)

        @block.vector
        def _(dve):
            step = [0]

            def link(ins):
                step[0] += 1
                ins.then_inc(s_dv, 1)
                dve.wait_ge(s_dv, step[0])

            def statistics(g):
                dve.wait_ge(s_x[g], 16)
                for j in range(4 * g, 4 * g + 4):
                    ins = dve.bn_stats(bn6[:, j, :], x_sb[:, j, :])
                link(ins)
                for j in range(4 * g, 4 * g + 4):
                    ins = dve.bn_aggr(mv[:, j, :], bn6[:, j, :])
                link(ins)
                dve.tensor_scalar(ve[:, 4 * g:4 * g + 4], mv[:, 4 * g:4 * g + 4, 1], LN_EPS, None, ALU.add)\
                    .then_inc(s_var, 1)

            def rsqrt(y, root, v, t):
                link(dve.reciprocal(y, root))
                link(dve.tensor_tensor(t, y, y, ALU.mult))
                link(dve.tensor_tensor(t, t, v, ALU.mult))
                link(dve.tensor_scalar(t, t, -0.5, 1.5, ALU.mult, ALU.add))
                return dve.tensor_tensor(y, y, t, ALU.mult)

            def normalise(g):
                dve.wait_ge(s_sd, g + 1)
                a = slice(4 * g, 4 * g + 4)
                link(rsqrt(rs[:, a], sd[:, a], ve[:, a], nt[:, a]))
                for j in range(4 * g, 4 * g + 4):
                    ins = dve.tensor_scalar(ROWS[:, j, 0:H], x_sb[:, j, :], mv[:, j, 0:1], rs[:, j:j + 1],
                                            ALU.subtract, ALU.mult)
                ins.then_inc(s_xn, 1)

            for g in range(QB):
                statistics(g)
                normalise(g)
            dve.wait_ge(s_cst, 32)
            dve.tensor_copy(identb[:, :], ident).then_inc(s_cb, 1)
            dve.tensor_copy(maskb[:, :], late_c[:, 0:P]).then_inc(s_cb, 1)

            dve.wait_ge(s_g, 48)
            dve.tensor_scalar(gs[:, 0:1], gq[:, 0:1], SCALE, None, ALU.mult).then_inc(s_cb, 1)
            dve.tensor_scalar(gs[0:64, 1:2], gq[0:64, 1:2], SCALE, None, ALU.mult).then_inc(s_cb, 1)

            for j in range(NB):
                dve.wait_ge(s_al, j + 1)
                dve.max(M8[:, j, :], AL[:, j, A_RT:A_W])
                ins = dve.tensor_tensor_reduce(out=kv_junk, in0=AL[:, j, A_KV:A_PE], in1=AL[:, j, A_KV:A_PE],
                                               scale=1.0, scalar=0.0, op0=ALU.mult, op1=ALU.add,
                                               accum_out=ssq[:, 1, j:j + 1])
                link(ins)
            dve.wait_ge(s_ssq, NB)
            dve.tensor_scalar(rv[:, 0, :], ssq[:, 0, :], 1.0 / RQ, RMS_EPS, ALU.mult, ALU.add).then_inc(s_rv, 1)
            dve.tensor_scalar(rv[:, 1, :], ssq[:, 1, :], 1.0 / RK, RMS_EPS, ALU.mult, ALU.add).then_inc(s_rv, 1)

            for j in range(NB):
                ins = dve.match_replace(LR[:, j, :], M8[:, j, :], AL[:, j, A_RT:A_W], -3e38)
            link(ins)

            dve.wait_ge(s_rsd, 1)
            rsqrt(rr, rsd, rv, rt).then_inc(s_rr, 1)
            dve.wait_ge(s_rr, 1)
            def low_scaled(dst, src, scale, high):
                return dve.scalar_tensor_tensor(out=dst, in0=src, scalar=scale, in1=high, op0=ALU.mult,
                                                op1=ALU.subtract)

            def values_out_low(n):
                dve.wait_ge(s_hivo, n + 1)
                dve.tensor_tensor(WVO[:, 1, n, :], bank[:, n % 2, 0:H], WVO[:, 0, n, :], ALU.subtract)\
                    .then_inc(s_lovo, 1)

            def combined_low(m):
                a = slice(8 * m, 8 * m + 8)
                c = 6 - 4 * m
                dve.wait_ge(s_hic, 2 * m + 2)
                low_scaled(heads(WC0[:, 1, :])[:, a, 0:64], heads(bank[:, c, :], 8), gs[:, 0:1],
                           heads(WC0[:, 0, :])[:, a, 0:64]).then_inc(s_loc, 1)
                low_scaled(heads(WC1)[64:P, a, 0:64], heads(bank[0:64, c + 1, :], 8), gs[0:64, 1:2],
                           heads(WC1)[0:64, a, 0:64]).then_inc(s_loc, 1)

            values_out_low(0)
            for j in range(NB):
                ins = dve.scalar_tensor_tensor(out=V[:, j, :], in0=AL[:, j, A_KV:A_PE], scalar=rr[:, 1, j:j + 1],
                                               in1=gkv, op0=ALU.mult, op1=ALU.mult)
            ins.then_inc(s_v, 1)
            values_out_low(1)
            logits = AL[:, :, A_RT:A_W]
            dve.tensor_tensor(SEL, LR, logits, ALU.not_equal).then_inc(s_sel, 1)
            dve.tensor_tensor(EX, logits, M8[:, :, 0:1].broadcast_to([P, NB, E]), ALU.subtract).then_inc(s_sub, 1)
            for n in range(2, 4):
                values_out_low(n)
            combined_low(0)
            values_out_low(4)
            dve.wait_ge(s_ex, 1)
            dve.wait_ge(s_sel, 1)
            link(dve.tensor_reduce(den[:, 0, :], EX, AX.X, ALU.add))
            values_out_low(5)
            link(dve.tensor_tensor(EX, EX, SEL, ALU.mult))
            link(dve.tensor_reduce(den[:, 1, :], EX, AX.X, ALU.add))
            link(dve.scalar_tensor_tensor(out=den[:, 2, :], in0=den[:, 0, :], scalar=1e-20, in1=den[:, 1, :],
                                          op0=ALU.mult, op1=ALU.add))
            dve.reciprocal(den[:, 0, :], den[:, 2, :]).then_inc(s_den, 1)
            values_out_low(6)
            dve.wait_ge(s_pehi, 2)
            low_scaled(heads(WC0[:, 1, :])[:, :, 64:P], WQ0[:, :, NOPE:RQ], gs[:, 0:1],
                       heads(WC0[:, 0, :])[:, :, 64:P]).then_inc(s_pelo, 1)
            low_scaled(heads(WC1)[64:P, :, 64:P], WQ1[0:64, :, NOPE:RQ], gs[0:64, 1:2],
                       heads(WC1)[0:64, :, 64:P]).then_inc(s_pelo, 1)
            values_out_low(7)
            combined_low(1)

            for g in range(QB):
                dve.wait_ge(s_khi, g + 1)
                cols = slice(g * S, (g + 1) * S)
                dve.tensor_tensor(KT[:, 1, cols], bank[:, 4 + g, :], KT[:, 0, cols], ALU.subtract).then_inc(s_klo, 1)
            for g in range(QB):
                for c in range(2):
                    n = 2 * g + c
                    dve.wait_ge(s_qahi, n + 1)
                    cols = slice(g * S, (g + 1) * S)
                    dve.tensor_tensor(QA[:, 2 * c + 1, cols], bank[:, 4 + n % 4, :], QA[:, 2 * c, cols],
                                      ALU.subtract).then_inc(s_qalo, 1)

            def rotate(g, m):
                i = (m // 4) % QB
                pe = heads(bank[:, m % 4, :], 4)[:, :, 64:P]
                sin = cst[:, C_SIN + i * 64:C_SIN + (i + 1) * 64].unsqueeze(1).broadcast_to([P, 4, ROPE])
                halves = "p h (a n) -> p h a n"
                dve.wait_ge(s_proj, g + 1)
                after(dve, s_rope, g - 3)
                dve.tensor_tensor(RT[m % 4].rearrange(halves, a=2), pe.rearrange(halves, a=2)[:, :, ::-1, :],
                                  sin.rearrange(halves, a=2), ALU.mult).then_inc(s_ropa, 1)

            def q_low(g, b, m):
                dve.wait_ge(s_qhi, g + 1)
                n, cols = m % 4, slice((m // 4) * P, (m // 4 + 1) * P)
                q = [Q[:, one(b), 2 * n:2 * n + 2, :, l, cols].rearrange("p a h s q -> p (a h s) q") for l in range(2)]
                dve.tensor_tensor(q[1], heads(bank[:, 4 + n, :], 4), q[0], ALU.subtract).then_inc(s_qlo, 1)

            def first_of_halves(n, half):
                after(dve, s_tk, 3 * n + half)
                dve.tensor_copy(small[0:1, 48 + half:49 + half], cst[0:1, 0:1])
                if half == 0:
                    dve.max(EIGHT[:, :], KEYT).then_inc(s_tk, 1)
                else:
                    dve.match_replace(KEYT, EIGHT[:, :], KEYT, 0.0).then_inc(s_tk, 1)
                    dve.tensor_copy(KM[:, bass.ds(n * 8, 8)], EIGHT[:, :]).then_inc(s_tk, 1)

            def first_of_all(n):
                if n == 0:
                    dve.wait_ge(s_tk, 3 * ROUNDS)
                    dve.tensor_copy(KM[0:E, 8 * ROUNDS:], KM[E:P, 0:CAP]).then_inc(s_tk, 1)
                dve.wait_ge(s_tk, 3 * ROUNDS + 1 + n)
                dve.max(K64[:, 8 * n:8 * n + 8], KM[0:E, :]).then_inc(s_first, 1)
                if n < 7:
                    dve.wait_ge(s_first, n + 1)
                    dve.match_replace(KM[0:E, :], K64[:, 8 * n:8 * n + 8], KM[0:E, :], 0.0).then_inc(s_tk, 1)

            def row_numbers():
                dve.wait_ge(s_kx, 32)
                dve.tensor_scalar(EMPTY[:, :], KX[:, :], 0.0, cst[:, C_SLOT:C_SLOT + 1], ALU.is_equal, ALU.mult)
                link(dve.tensor_scalar(ROWNO[:, :], KX[:, :], -1.0, float(T), ALU.mult, ALU.add))
                link(dve.tensor_tensor(ROWNO[:, :], ROWNO[:, :], EMPTY[:, :], ALU.add))

            def indices(q, p):
                after(dve, s_add, (p - 3) * 16)
                dve.tensor_tensor(idx[:, 2 * q:2 * q + 2], ROWNO[:, one(p)].broadcast_to([P, 2]),
                                  cst[:, C_OFF:C_OFF + 2], ALU.add).then_inc(s_no, 1)

            def queries(b, last):
                for m in range(16):
                    g = b * 16 + m
                    if not last or m + 2 < 16:
                        rotate(g + 2, m + 2)
                    if last and m == 15:
                        row_max(0, 0)
                    if m > 0:
                        q_low(g - 1, b, m - 1)
                    if not last and m % 5 in (1, 3):
                        first_of_halves(b * 3 + m // 5, m % 5 // 2)
                    if last and m < 8:
                        first_of_all(m)
                    if last and m == 11:
                        row_numbers()
                        for q in range(2):
                            indices(q, q)
                if last:
                    row_max(1, 1)
                q_low(b * 16 + 15, b, 15)


            def row_max(g, u):
                _, i = unit(u % UNITS)
                dve.wait_ge(s_sc, g + 1)
                x = 2 * (u % 2)
                dve.tensor_reduce(nmax[:, u % 4, :], bank[:, x:x + 2, 0:(i + 1) * P], AX.X, ALU.max, negate=True)\
                    .then_inc(s_max, 1)

            def recip(g, u):
                _, i = unit(u % UNITS)
                dve.wait_ge(s_exp, g + 1)
                dve.reciprocal(rinv[:, u % 4, :], sums[:, u % 4, :]).then_inc(s_rin, 1)
                if i in DVE_NORM:
                    t = PR[u % 4][:, 1, 0:(i + 1) * P]
                    dve.wait_ge(s_rin, g + 1)
                    dve.tensor_scalar(t, t, rinv[:, u % 4, 1:2], None, ALU.mult).then_inc(s_nrmv, 1)

            def pt_out(g, u):
                _, i = unit(u % UNITS)
                nk = (i + 1) * P
                dve.wait_ge(s_pt[0], g + 1)
                dve.tensor_copy(PT[u % 2][:, 0, 0:nk], bank[:, 4, 0:nk]).then_inc(s_pte[0], 1)

            def o_low(g, hp, u):
                b, i = unit(u)
                dve.wait_ge(s_ohi, g + 1)
                o = [Q[:, b, one(hp), 0, l, i * P:(i + 1) * P].rearrange("p a q -> p (a q)") for l in range(2)]
                dve.tensor_tensor(o[1], bank[:, 6, 0:P], o[0], ALU.subtract).then_inc(s_olo, 1)

            def experts(g, hp, u, last):
                q, f = u // 4, u % 4
                p = hp * 4 + q
                if f == 0:
                    after(dve, s_add, p * 16 - 16)
                    if not (last and q == 3) and not (isinstance(hp, int) and hp == 0 and q == 0):
                        indices((q + 1) % 4, p + 1)
                if f == 1:
                    dve.wait_ge(s_eg, p + 1)
                    dve.tensor_scalar(D1, EG, 1.0, None, ALU.add).then_inc(s_hd, 1)
                    dve.wait_ge(s_hd, p * 3 + 1)
                    dve.reciprocal(RG, D1).then_inc(s_hd, 1)
                    dve.wait_ge(s_hd, p * 3 + 2)
                    dve.tensor_tensor(GR, bank[:, 7, 0:F], RG, ALU.mult).then_inc(s_hd, 1)
                    dve.wait_ge(s_hd, p * 3 + 3)
                    dve.tensor_tensor(HM, bank[:, 7, F:2 * F], GR, ALU.mult).then_inc(s_hm, 1)
                if f == 3:
                    dve.wait_ge(s_f, g + 1)
                    dve.wait_ge(s_wc[q % 2], (hp * 2 + q // 2) * 32 + 32)
                    dve.tensor_scalar(Y[q % 2], bank[:, 7, 0:H], WCOL[q % 2], None, ALU.mult).then_inc(s_y, 1)

            dve.wait_ge(s_rowsd, 48)
            rotate(0, 0)
            rotate(1, 1)
            dve.wait_ge(s_key, 1)
            queries(0, False)
            with dve.Fori(1, B - 1) as b:
                queries(b, False)
            queries(B - 1, True)

            recip(0, 0)
            recip(1, 1)
            row_max(2, 2)
            pt_out(0, 0)

            def attend(hp, last):
                for u in range(UNITS):
                    g = hp * UNITS + u
                    if u > 0:
                        o_low(g - 1, hp, u - 1)
                    experts(g, hp, u, last)
                    if not last or u + 3 < UNITS:
                        row_max(g + 3, u + 3)
                    if not last or u + 2 < UNITS:
                        recip(g + 2, u + 2)
                    if not last or u + 1 < UNITS:
                        pt_out(g + 1, u + 1)
                o_low(hp * UNITS + UNITS - 1, hp, UNITS - 1)

            attend(0, False)
            with dve.Fori(1, HP - 1) as hp:
                attend(hp, False)
            attend(HP - 1, True)

            def finish(b, n):
                j = b * 4 + n
                dve.wait_ge(s_fin, j + 1)
                dve.wait_ge(s_base, j * 2 + 2)
                after(dve, s_out[n], b * 16)
                dve.tensor_tensor(OUT[n], bank[:, n, 0:H], XR[n], ALU.add).then_inc(s_o, 1)

            for n in range(4):
                finish(0, n)
            with dve.Fori(1, B) as b:
                for n in range(4):
                    finish(b, n)

        @block.tensor
        def _(pe):
            pe.wait_ge(s_cst, 32)
            pe.wait_ge(s_wa, 48)
            for c in range(NC):
                ins = pe.transpose(bank[:, 2, c * E:(c + 1) * E], rt_row[0:E, c * P:(c + 1) * P], ident[0:E, 0:E])
            ins.then_inc(s_rt, 1)

            def x_t(g):
                pe.wait_ge(s_xn, g + 1)
                for c in range(NC):
                    if g >= 1:
                        pe.wait_ge(s_xte, (g - 1) * NC + c + 1)
                    for n in range(4):
                        ins = pe.transpose(bank[:, c, n * P:(n + 1) * P], ROWS[:, 4 * g + n, c * P:(c + 1) * P], ident)
                    ins.then_inc(s_xt, 1)

            def first(j):
                pe.wait_ge(s_xte, (j // 4 + 1) * NC)
                if j >= 2:
                    pe.wait_ge(s_al, j - 1)
                for c in range(NC):
                    ins = pe.matmul(bank[:, 2 + j % 2, 0:W_W], xnT[:, c, j * P:(j + 1) * P], WA[:, c, :],
                                    start=(c == 0), stop=(c == NC - 1))
                ins.then_inc(s_a, 1)

            x_t(0)
            pe.wait_ge(s_rte, 1)
            for g in range(QB):
                for n in range(4):
                    if n == 2 and g + 1 < QB:
                        x_t(g + 1)
                    first(4 * g + n)

            pe.wait_ge(s_whead, 48)

            def head_t(hd):
                if hd >= 2:
                    pe.wait_ge(s_wte, hd - 1)
                o = bank[:, 4 + hd % 2, :]
                pe.transpose(o[:, 0:P], WQ0[:, hd, 0:NOPE], ident)
                pe.transpose(o[:, P:RQ], WQ1[0:64, hd, 0:NOPE], ident[0:64, 0:64])
                pe.transpose(o[:, RQ:256], WKV[0:64, hd, 0:NOPE], ident[0:64, 0:64])
                pe.transpose(o[:, 256:320], WKV[0:64, hd, NOPE:256], ident[0:64, 0:64]).then_inc(s_wt, 1)

            def head_products(hd):
                pe.wait_ge(s_wte, hd + 1)
                if hd == 0:
                    pe.wait_ge(s_wo, 16)
                w, n, k = WT[hd % 2], hd // 2, hd % 8
                c = 6 - 4 * (hd // 8)
                pe.matmul(bank[:, c, k * 64:(k + 1) * 64], w[:, 0:P], w[:, RQ:256], start=True, stop=True)
                ins = pe.matmul(bank[0:64, c + 1, k * 64:(k + 1) * 64], w[:, P:RQ], w[:, RQ:256], start=True, stop=True)
                if k == 7:
                    ins.then_inc(s_cmb, 1)
                if n >= 2 and hd % 2 == 0:
                    pe.wait_ge(s_lovo, n - 1)
                r = 64 * (hd % 2)
                pe.matmul(bank[r:r + 64, n % 2, 0:H], w[:, 256:320], WO[:, hd, :], start=True, stop=True)\
                    .then_inc(s_vo, 1)

            head_t(0)
            for hd in range(NH):
                if hd + 1 < NH:
                    head_t(hd + 1)
                head_products(hd)

            pe.wait_ge(s_kr, 2)
            pe.wait_ge(s_wte, NH)
            for g in range(QB):
                if g == 2:
                    pe.wait_ge(s_loc, 2)
                for n in range(4):
                    ins = pe.transpose(bank[:, 4 + g, n * P:(n + 1) * P], KR[:, 4 * g + n, :], ident)
                ins.then_inc(s_kt, 1)
            pe.wait_ge(s_qan, NB)

            def qa_t(m):
                g, c = m // 2, m % 2
                if m < 4:
                    pe.wait_ge(s_klo, m + 1)
                else:
                    pe.wait_ge(s_qalo, m - 3)
                for n in range(4):
                    a0 = 0 if c == 0 else P
                    ins = pe.transpose(bank[:, 4 + m % 4, n * P:(n + 1) * P], AL[:, 4 * g + n, a0:a0 + P], ident)
                ins.then_inc(s_qa, 1)

            for m in range(2):
                qa_t(m)
            pe.wait_ge(s_selk, 2)
            pe.wait_ge(s_loc, 4)
            for j in range(NB // 2):
                ins = pe.transpose(bank[:, 2 + j // 4, (j % 4) * P:(j % 4 + 1) * P],
                                   SELK[:, j, :, :].rearrange("p a e -> p (a e)"), ident)
            ins.then_inc(s_selt, 1)

            def project(g, b, m):
                j = b * 4 + m // 4
                n = m % 4
                after(pe, s_nope, g - 3)
                w = [WC0[:, 0, n * S:(n + 1) * S], WC0[:, 1, n * S:(n + 1) * S], WC1[:, n * S:(n + 1) * S]]
                for k, (a, c) in enumerate(((0, 0), (0, 1), (1, 0), (2, 2), (3, 2))):
                    x = QA[:, a, bass.ds(j * P, P)]
                    ins = pe.matmul(bank[:, n, :], x, w[c], start=(k == 0), stop=(k == 4))
                ins.then_inc(s_proj, 1)

            def q_t(g, m):
                pe.wait_ge(s_rope, g + 1)
                after(pe, s_qlo, g - 3)
                for k in range(4):
                    ins = pe.transpose(bank[:, 4 + m % 4, k * P:(k + 1) * P], QR[m % 4][:, k, :], ident)
                ins.then_inc(s_qt, 1)

            def queries(b, last):
                for m in range(16):
                    g = b * 16 + m
                    if not last or m + 3 < 16:
                        project(g + 3, b if m + 3 < 16 else b + 1, (m + 3) % 16)
                    if last and m >= 14:
                        pe.wait_ge(s_nope, 4 * NB - 2 * (15 - m))
                        scores(m - 14, 0, m - 14)
                    q_t(g, m)


            def scores(g, hp, u):
                b, i = unit(u)
                nk = (i + 1) * P
                after(pe, s_exp, g - 1)
                for s in range(2):
                    o = bank[:, 2 * (u % 2) + s, :]
                    q = [Q[:, b, one(hp), s, l, i * P:nk].rearrange("p a q -> p (a q)") for l in range(2)]
                    k = [KT[:, l, b * S:b * S + nk] for l in range(2)]
                    pe.matmul(o[:, 0:nk], q[0], k[0], start=True, stop=False)
                    pe.matmul(o[:, 0:nk], q[0], k[1], start=False, stop=False)
                    pe.matmul(o[:, 0:nk], q[1], k[0], start=False, stop=False)
                    ins = pe.matmul(o[:, i * P:nk], identb[:, :], maskb[:, :], start=False, stop=True)
                ins.then_inc(s_sc, 1)

            def probs_t(g, u, four):
                _, i = unit(u)
                done = sum(n in DVE_NORM for n in IORDER[:u % 4 + 1])
                for s in range(2):
                    if s == 0:
                        pe.wait_ge(s_nrm[0], g + 1)
                    elif i in DVE_NORM:
                        pe.wait_ge(s_nrmv, four * len(DVE_NORM) + done)
                    else:
                        pe.wait_ge(s_nrm[1], four * (4 - len(DVE_NORM)) + u % 4 + 1 - done)
                    after(pe, s_pte[s], g)
                    for k in range(i + 1):
                        ins = pe.transpose(bank[:, 4 + s, k * P:(k + 1) * P], PR[u % 4][:, s, k * P:(k + 1) * P], ident)
                    ins.then_inc(s_pt[s], 1)

            def values(g, u):
                b, i = unit(u)
                for s in range(2):
                    pe.wait_ge(s_pte[s], g + 1)
                after(pe, s_olo, g)
                for k in range(i + 1):
                    for s in range(2):
                        ins = pe.matmul(bank[64 * s:64 * s + 64, 6, 0:P], V[:, b * QB + k, :],
                                        PT[u % 2][:, s, k * P:(k + 1) * P], start=(k == 0), stop=(k == i))
                ins.then_inc(s_pv, 1)

            def experts(g, hp, u):
                q, f = u // 4, u % 4
                p = hp * 4 + q
                if f == 0:
                    pe.wait_ge(s_xb[q % 2], (hp * 2 + q // 2) * 16 + 16)
                    after(pe, s_y, p)
                    for c in range(NC):
                        ins = pe.transpose(bank[:, 7, c * P:(c + 1) * P], XB[q % 2][:, c:H:NC], ident)
                if f == 1:
                    pe.wait_ge(s_xbt, p + 1)
                    pe.wait_ge(s_w[q], hp * 48 + 48)
                    for c in range(NC):
                        for e in range(2):
                            r = 64 * e
                            ins = pe.matmul(bank[r:r + 64, 7, 0:2 * F].rearrange("p (g n) -> p g n", g=2),
                                            XBT[:, c, r:r + 64], WGU[q][:, e, :, c * F:(c + 1) * F],
                                            start=(c == 0), stop=(c == NC - 1))
                if f == 2:
                    pe.wait_ge(s_hm, p + 1)
                    ins = pe.transpose(bank[0:F, 7, 0:P], HM, ident)
                if f == 3:
                    pe.wait_ge(s_hmt, p + 1)
                    for e in range(2):
                        r = 64 * e
                        ins = pe.matmul(bank[r:r + 64, 7, 0:H], HMT[0:F, r:r + 64], WD[q][0:F, e, :], start=True,
                                        stop=True)
                ins.then_inc(s_f, 1)

            pe.wait_ge(s_cb, 2)
            pe.wait_ge(s_lovo, HP)
            pe.wait_ge(s_pelo, 2)
            pe.wait_ge(s_qalo, 2)
            project(0, 0, 0)
            project(1, 0, 1)
            for m in range(2, 2 * QB):
                qa_t(m)
            pe.wait_ge(s_key, 1)
            project(2, 0, 2)
            pe.wait_ge(s_qalo, 2 * QB)
            queries(0, False)
            with pe.Fori(1, B - 1) as b:
                queries(b, False)
            queries(B - 1, True)

            pe.wait_ge(s_qlo, 4 * NB)
            scores(2, 0, 2)
            probs_t(0, 0, 0)

            def attend(hp, last):
                for u in range(UNITS):
                    g = hp * UNITS + u
                    experts(g, hp, u)
                    if not last or u + 3 < UNITS:
                        scores(g + 3, hp if u + 3 < UNITS else hp + 1, (u + 3) % UNITS)
                    if not last or u + 1 < UNITS:
                        probs_t(g + 1, (u + 1) % UNITS, hp * 4 + (u + 1) // 4)
                    values(g, u)

            attend(0, False)
            with pe.Fori(1, HP - 1) as hp:
                attend(hp, False)
            attend(HP - 1, True)

            def project_out(b, n):
                after(pe, s_o, b * 4 + n - 3)
                for hp in range(HP):
                    o = [Q[:, one(b), hp, 0, l, n * P:(n + 1) * P].rearrange("p a q -> p (a q)") for l in range(2)]
                    for k, (x, w) in enumerate(((0, 0), (0, 1), (1, 0))):
                        ins = pe.matmul(bank[:, n, 0:H], o[x], WVO[:, w, hp, :], start=(hp == 0 and k == 0),
                                        stop=(hp == HP - 1 and k == 2))
                ins.then_inc(s_fin, 1)

            pe.wait_ge(s_exp, UNITS * HP)
            pe.wait_ge(s_olo, UNITS * HP)
            for n in range(4):
                project_out(0, n)
            with pe.Fori(1, B) as b:
                for n in range(4):
                    project_out(b, n)


_INS = ['L0_attn_h', 'L0_attn_w_q_a', 'L0_attn_g_q_a', 'L0_attn_w_q_b', 'L0_attn_w_kv_a', 'L0_attn_g_kv_a',
        'L0_attn_w_kv_b', 'L0_attn_w_o', 'L0_ffn_router_w', 'L0_ffn_w_gate', 'L0_ffn_w_up', 'L0_ffn_w_down']
_OUTS = [((B, S, H), 'float32')]


def kernel(**inputs):
    import numpy as _np
    import concourse.bacc as _bacc
    from concourse import mybir as _mybir
    from concourse.bass_utils import run_bass_kernel_spmd as _run

    nc = _bacc.Bacc("TRN2", target_bir_lowering=False, num_devices=1)
    arrays, args = {}, []
    for name in _INS:
        a = _np.ascontiguousarray(inputs[name])
        arrays[f"in_{name}_dram"] = a
        args.append(nc.dram_tensor(f"in_{name}_dram", a.shape, _mybir.dt.from_np(a.dtype), kind="ExternalInput").ap())
    arrays["constants_dram"] = table()
    args.append(nc.dram_tensor("constants_dram", (P, C_W), F32, kind="ExternalInput").ap())
    for i, (shape, dtype) in enumerate(_OUTS):
        dt = _mybir.dt.from_np(_np.dtype(dtype))
        args.append(nc.dram_tensor(f"out_{i}_dram", shape, dt, kind="ExternalOutput").ap())
    mla_moe_kernel(nc, *args)
    r = _run(nc, [arrays], core_ids=[0])
    got = tuple(r.results[0][f"out_{i}_dram"] for i in range(len(_OUTS)))
    return got[0]
```
